# Optimizing a Trainium2 kernel written in Bass

```python
import numpy as np
import jax
import jax.numpy as jnp

def _softmax(x, axis=-1):
    return jax.nn.softmax(x, axis=axis)

def _gelu(x):
    return jax.nn.gelu(x, approximate=True)

def _silu(x):
    return jax.nn.silu(x)

def _sigmoid(x):
    return jax.nn.sigmoid(x)

def _layernorm(x, axis=-1, eps=1e-05):
    m = jnp.mean(x, axis=axis, keepdims=True)
    v = jnp.var(x, axis=axis, keepdims=True)
    return (x - m) / jnp.sqrt(v + eps)

def _scatter_add(tgt, idx, src, axis=0):
    return tgt.at[idx].add(src)

def _segment_sum(src, seg, n):
    return jax.ops.segment_sum(src, seg, n)
kernel_name = 'mk_hybrid_d1_jaxref_r8_848a8b'

def setup_inputs(seed: int=0):
    np.random.seed(seed)
    _w = jnp.asarray

    def _L0_attn_a_setup():
        import jax, jax.numpy as jnp
        import numpy as np
        N_KV_HEAD = 8
        GROUP_SIZE = 4
        ROPE_BASE = 10000.0

        def _rope(x):
            t, d = (x.shape[-2], x.shape[-1])
            j = jnp.arange(d // 2, dtype=jnp.float32)
            theta = jnp.asarray(ROPE_BASE, jnp.float32) ** (-2.0 * j / d)
            pos = (jnp.arange(t, dtype=jnp.float32) + 1.0)[:, None]
            ang = pos * theta[None, :]
            C = jnp.concatenate([ang, ang], axis=-1)
            x2 = jnp.concatenate([-x[..., d // 2:], x[..., :d // 2]], axis=-1)
            return x * jnp.cos(C) + x2 * jnp.sin(C)
        key = jax.random.key(seed)
        ks = jax.random.split(key, 9)
        b, t, e = (2, 256, 256)
        kv = e // GROUP_SIZE
        s_in = 1.0 / np.sqrt(e)
        return {'x': jax.random.normal(ks[0], (b, t, e), jnp.float32), 'Wq': jax.random.normal(ks[1], (e, e), jnp.float32) * s_in, 'bq': jax.random.normal(ks[2], (e,), jnp.float32) * 0.01, 'Wk': jax.random.normal(ks[3], (kv, e), jnp.float32) * s_in, 'bk': jax.random.normal(ks[4], (kv,), jnp.float32) * 0.01, 'Wv': jax.random.normal(ks[5], (kv, e), jnp.float32) * s_in, 'bv': jax.random.normal(ks[6], (kv,), jnp.float32) * 0.01, 'Wo': jax.random.normal(ks[7], (e, e), jnp.float32) * s_in, 'bo': jax.random.normal(ks[8], (e,), jnp.float32) * 0.01}
    _L0_attn_a_in = _L0_attn_a_setup()

    def _L0_attn_b_setup():
        import jax, jax.numpy as jnp
        import numpy as np
        import math
        EMBED_DIM = 256
        NUM_HEADS = 16
        DEPTH = 12
        HEAD_DIM = EMBED_DIM // NUM_HEADS // 2
        LAMBDA_INIT = 0.8 - 0.6 * math.exp(-0.3 * DEPTH)

        def _diff_attn(query, Wq, Wk, Wv, Wo, lq1, lk1, lq2, lk2, g):
            B, T, E = query.shape
            H, D = (NUM_HEADS, HEAD_DIM)
            S = T
            scaling = D ** (-0.5)
            q = (query @ Wq.T).reshape(B, T, 2 * H, D).transpose(0, 2, 1, 3)
            k = (query @ Wk.T).reshape(B, S, 2 * H, D).transpose(0, 2, 1, 3)
            v = (query @ Wv.T).reshape(B, S, H, 2 * D).transpose(0, 2, 1, 3)
            q = q * scaling
            attn = jnp.einsum('bhtd,bhsd->bhts', q, k)
            attn = jnp.nan_to_num(attn)
            causal = jnp.triu(jnp.full((T, S), -jnp.inf, attn.dtype), k=1)
            attn = jax.nn.softmax(attn + causal, axis=-1)
            lam1 = jnp.exp(jnp.sum(lq1 * lk1))
            lam2 = jnp.exp(jnp.sum(lq2 * lk2))
            lam = lam1 - lam2 + LAMBDA_INIT
            attn = attn.reshape(B, H, 2, T, S)
            attn = attn[:, :, 0] - lam * attn[:, :, 1]
            out = jnp.einsum('bhts,bhsd->bhtd', attn, v)
            rms = jax.lax.rsqrt(jnp.mean(out * out, axis=-1, keepdims=True) + 1e-05)
            out = out * rms * g
            out = out * (1.0 - LAMBDA_INIT)
            out = out.transpose(0, 2, 1, 3).reshape(B, T, H * 2 * D)
            return out @ Wo.T
        key = jax.random.key(seed)
        ks = jax.random.split(key, 9)
        B, T, E = (2, 256, EMBED_DIM)
        s = 1.0 / math.sqrt(E)
        return {'query': jax.random.normal(ks[0], (B, T, E), jnp.float32), 'Wq': jax.random.normal(ks[1], (E, E), jnp.float32) * s, 'Wk': jax.random.normal(ks[2], (E, E), jnp.float32) * s, 'Wv': jax.random.normal(ks[3], (E, E), jnp.float32) * s, 'Wo': jax.random.normal(ks[4], (E, E), jnp.float32) * s, 'lambda_q1': jax.random.normal(ks[5], (HEAD_DIM,), jnp.float32) * 0.1, 'lambda_k1': jax.random.normal(ks[6], (HEAD_DIM,), jnp.float32) * 0.1, 'lambda_q2': jax.random.normal(ks[7], (HEAD_DIM,), jnp.float32) * 0.1, 'lambda_k2': jax.random.normal(ks[8], (HEAD_DIM,), jnp.float32) * 0.1, 'subln_weight': jnp.ones((2 * HEAD_DIM,), jnp.float32)}
    _L0_attn_b_in = _L0_attn_b_setup()

    def _L0_ffn_setup():
        import jax, jax.numpy as jnp
        import numpy as np
        DIM = 256
        INTER = 176
        E = 16
        TOPK = 4
        G = 4
        TOPK_G = 2
        N_SHARED = 2
        SHARED_INTER = N_SHARED * INTER
        ROUTE_SCALE = 1.0

        def _moe_forward(x, Wg, W1, W3, W2, Ws1, Ws3, Ws2):
            B, S, D = x.shape
            xt = x.reshape(-1, D)
            T = xt.shape[0]
            scores = jax.nn.softmax(xt @ Wg.T, axis=-1)
            sg = scores.reshape(T, G, E // G)
            group_scores = sg.max(axis=-1)
            gidx = jax.lax.top_k(group_scores, TOPK_G)[1]
            gmask = jax.nn.one_hot(gidx, G, dtype=jnp.float32).sum(axis=1) > 0
            masked = jnp.where(gmask[:, :, None], sg, -jnp.inf).reshape(T, E)
            topi = jax.lax.top_k(masked, TOPK)[1]
            weights = jnp.take_along_axis(scores, topi, axis=1) * ROUTE_SCALE
            combine = jnp.zeros((T, E), xt.dtype).at[jnp.arange(T)[:, None], topi].add(weights)
            h = jax.nn.silu(jnp.einsum('td,eid->eti', xt, W1)) * jnp.einsum('td,eid->eti', xt, W3)
            expert_out = jnp.einsum('eti,edi->etd', h, W2)
            y = jnp.einsum('etd,te->td', expert_out, combine)
            z = jax.nn.silu(xt @ Ws1.T) * (xt @ Ws3.T) @ Ws2.T
            return (y + z).reshape(B, S, D)
        key = jax.random.key(seed)
        ks = jax.random.split(key, 8)
        s = 0.02
        x = jax.random.normal(ks[0], (1, 256, DIM), dtype=jnp.float32)
        Wg = jax.random.normal(ks[1], (E, DIM), dtype=jnp.float32) * s
        W1 = jax.random.normal(ks[2], (E, INTER, DIM), dtype=jnp.float32) * s
        W3 = jax.random.normal(ks[3], (E, INTER, DIM), dtype=jnp.float32) * s
        W2 = jax.random.normal(ks[4], (E, DIM, INTER), dtype=jnp.float32) * s
        Ws1 = jax.random.normal(ks[5], (SHARED_INTER, DIM), dtype=jnp.float32) * s
        Ws3 = jax.random.normal(ks[6], (SHARED_INTER, DIM), dtype=jnp.float32) * s
        Ws2 = jax.random.normal(ks[7], (DIM, SHARED_INTER), dtype=jnp.float32) * s
        return {'x': x, 'Wg': Wg, 'W1': W1, 'W3': W3, 'W2': W2, 'Ws1': Ws1, 'Ws3': Ws3, 'Ws2': Ws2}
    _L0_ffn_in = _L0_ffn_setup()
    _d = {'L0_attn_a_x': _L0_attn_a_in['x'], 'L0_attn_a_Wq': _L0_attn_a_in['Wq'], 'L0_attn_a_bq': _L0_attn_a_in['bq'], 'L0_attn_a_Wk': _L0_attn_a_in['Wk'], 'L0_attn_a_bk': _L0_attn_a_in['bk'], 'L0_attn_a_Wv': _L0_attn_a_in['Wv'], 'L0_attn_a_bv': _L0_attn_a_in['bv'], 'L0_attn_a_Wo': _L0_attn_a_in['Wo'], 'L0_attn_a_bo': _L0_attn_a_in['bo'], 'L0_attn_b_Wq': _L0_attn_b_in['Wq'], 'L0_attn_b_Wk': _L0_attn_b_in['Wk'], 'L0_attn_b_Wv': _L0_attn_b_in['Wv'], 'L0_attn_b_Wo': _L0_attn_b_in['Wo'], 'L0_attn_b_lambda_q1': _L0_attn_b_in['lambda_q1'], 'L0_attn_b_lambda_k1': _L0_attn_b_in['lambda_k1'], 'L0_attn_b_lambda_q2': _L0_attn_b_in['lambda_q2'], 'L0_attn_b_lambda_k2': _L0_attn_b_in['lambda_k2'], 'L0_attn_b_subln_weight': _L0_attn_b_in['subln_weight'], 'L0_ffn_Wg': _L0_ffn_in['Wg'], 'L0_ffn_W1': _L0_ffn_in['W1'], 'L0_ffn_W3': _L0_ffn_in['W3'], 'L0_ffn_W2': _L0_ffn_in['W2'], 'L0_ffn_Ws1': _L0_ffn_in['Ws1'], 'L0_ffn_Ws3': _L0_ffn_in['Ws3'], 'L0_ffn_Ws2': _L0_ffn_in['Ws2']}
    _x0 = _d['L0_attn_a_x']
    _d['L0_attn_a_x'] = jax.random.normal(jax.random.fold_in(jax.random.key(seed), 1), (4, 512, 256), dtype=_x0.dtype)
    del _x0
    return _d

def reference(L0_attn_a_x, L0_attn_a_Wq, L0_attn_a_bq, L0_attn_a_Wk, L0_attn_a_bk, L0_attn_a_Wv, L0_attn_a_bv, L0_attn_a_Wo, L0_attn_a_bo, L0_attn_b_Wq, L0_attn_b_Wk, L0_attn_b_Wv, L0_attn_b_Wo, L0_attn_b_lambda_q1, L0_attn_b_lambda_k1, L0_attn_b_lambda_q2, L0_attn_b_lambda_k2, L0_attn_b_subln_weight, L0_ffn_Wg, L0_ffn_W1, L0_ffn_W3, L0_ffn_W2, L0_ffn_Ws1, L0_ffn_Ws3, L0_ffn_Ws2):

    def _L0_attn_a_ref(x, Wq, bq, Wk, bk, Wv, bv, Wo, bo):
        import jax, jax.numpy as jnp
        import numpy as np
        N_KV_HEAD = 8
        GROUP_SIZE = 4
        ROPE_BASE = 10000.0

        def _rope(x):
            t, d = (x.shape[-2], x.shape[-1])
            j = jnp.arange(d // 2, dtype=jnp.float32)
            theta = jnp.asarray(ROPE_BASE, jnp.float32) ** (-2.0 * j / d)
            pos = (jnp.arange(t, dtype=jnp.float32) + 1.0)[:, None]
            ang = pos * theta[None, :]
            C = jnp.concatenate([ang, ang], axis=-1)
            x2 = jnp.concatenate([-x[..., d // 2:], x[..., :d // 2]], axis=-1)
            return x * jnp.cos(C) + x2 * jnp.sin(C)
        b, t, e = x.shape
        h, g = (N_KV_HEAD, GROUP_SIZE)
        d = e // (h * g)
        q = x @ Wq.T + bq
        k = x @ Wk.T + bk
        v = x @ Wv.T + bv
        q = q.reshape(b, t, h, g, d).transpose(0, 3, 2, 1, 4)
        k = k.reshape(b, t, h, d).transpose(0, 2, 1, 3)
        v = v.reshape(b, t, h, d).transpose(0, 2, 1, 3)
        q = _rope(q)
        k = _rope(k)
        scale = jnp.asarray(np.sqrt(d), x.dtype)
        att = jnp.einsum('bghqd,bhkd->bghqk', q, k) / scale
        causal = jnp.tril(jnp.ones((t, t), bool))
        att = jnp.where(causal, att, -jnp.inf)
        att = jax.nn.softmax(att, axis=-1)
        y = jnp.einsum('bghqk,bhkd->bghqd', att, v)
        y = y.transpose(0, 3, 2, 1, 4).reshape(b, t, e)
        return y @ Wo.T + bo

    def _L0_attn_b_ref(query, Wq, Wk, Wv, Wo, lambda_q1, lambda_k1, lambda_q2, lambda_k2, subln_weight):
        import jax, jax.numpy as jnp
        import numpy as np
        import math
        EMBED_DIM = 256
        NUM_HEADS = 16
        DEPTH = 12
        HEAD_DIM = EMBED_DIM // NUM_HEADS // 2
        LAMBDA_INIT = 0.8 - 0.6 * math.exp(-0.3 * DEPTH)

        def _diff_attn(query, Wq, Wk, Wv, Wo, lq1, lk1, lq2, lk2, g):
            B, T, E = query.shape
            H, D = (NUM_HEADS, HEAD_DIM)
            S = T
            scaling = D ** (-0.5)
            q = (query @ Wq.T).reshape(B, T, 2 * H, D).transpose(0, 2, 1, 3)
            k = (query @ Wk.T).reshape(B, S, 2 * H, D).transpose(0, 2, 1, 3)
            v = (query @ Wv.T).reshape(B, S, H, 2 * D).transpose(0, 2, 1, 3)
            q = q * scaling
            attn = jnp.einsum('bhtd,bhsd->bhts', q, k)
            attn = jnp.nan_to_num(attn)
            causal = jnp.triu(jnp.full((T, S), -jnp.inf, attn.dtype), k=1)
            attn = jax.nn.softmax(attn + causal, axis=-1)
            lam1 = jnp.exp(jnp.sum(lq1 * lk1))
            lam2 = jnp.exp(jnp.sum(lq2 * lk2))
            lam = lam1 - lam2 + LAMBDA_INIT
            attn = attn.reshape(B, H, 2, T, S)
            attn = attn[:, :, 0] - lam * attn[:, :, 1]
            out = jnp.einsum('bhts,bhsd->bhtd', attn, v)
            rms = jax.lax.rsqrt(jnp.mean(out * out, axis=-1, keepdims=True) + 1e-05)
            out = out * rms * g
            out = out * (1.0 - LAMBDA_INIT)
            out = out.transpose(0, 2, 1, 3).reshape(B, T, H * 2 * D)
            return out @ Wo.T
        return _diff_attn(query, Wq, Wk, Wv, Wo, lambda_q1, lambda_k1, lambda_q2, lambda_k2, subln_weight)

    def _L0_ffn_ref(x, Wg, W1, W3, W2, Ws1, Ws3, Ws2):
        import jax, jax.numpy as jnp
        import numpy as np
        DIM = 256
        INTER = 176
        E = 16
        TOPK = 4
        G = 4
        TOPK_G = 2
        N_SHARED = 2
        SHARED_INTER = N_SHARED * INTER
        ROUTE_SCALE = 1.0

        def _moe_forward(x, Wg, W1, W3, W2, Ws1, Ws3, Ws2):
            B, S, D = x.shape
            xt = x.reshape(-1, D)
            T = xt.shape[0]
            scores = jax.nn.softmax(xt @ Wg.T, axis=-1)
            sg = scores.reshape(T, G, E // G)
            group_scores = sg.max(axis=-1)
            gidx = jax.lax.top_k(group_scores, TOPK_G)[1]
            gmask = jax.nn.one_hot(gidx, G, dtype=jnp.float32).sum(axis=1) > 0
            masked = jnp.where(gmask[:, :, None], sg, -jnp.inf).reshape(T, E)
            topi = jax.lax.top_k(masked, TOPK)[1]
            weights = jnp.take_along_axis(scores, topi, axis=1) * ROUTE_SCALE
            combine = jnp.zeros((T, E), xt.dtype).at[jnp.arange(T)[:, None], topi].add(weights)
            h = jax.nn.silu(jnp.einsum('td,eid->eti', xt, W1)) * jnp.einsum('td,eid->eti', xt, W3)
            expert_out = jnp.einsum('eti,edi->etd', h, W2)
            y = jnp.einsum('etd,te->td', expert_out, combine)
            z = jax.nn.silu(xt @ Ws1.T) * (xt @ Ws3.T) @ Ws2.T
            return (y + z).reshape(B, S, D)
        return _moe_forward(x, Wg, W1, W3, W2, Ws1, Ws3, Ws2)
    x = L0_attn_a_x
    x = x + _L0_attn_a_ref(_layernorm(x, axis=-1), L0_attn_a_Wq, L0_attn_a_bq, L0_attn_a_Wk, L0_attn_a_bk, L0_attn_a_Wv, L0_attn_a_bv, L0_attn_a_Wo, L0_attn_a_bo)
    x = x + _L0_ffn_ref(_layernorm(x, axis=-1), L0_ffn_Wg, L0_ffn_W1, L0_ffn_W3, L0_ffn_W2, L0_ffn_Ws1, L0_ffn_Ws3, L0_ffn_Ws2)
    x = x + _L0_attn_b_ref(_layernorm(x, axis=-1), L0_attn_b_Wq, L0_attn_b_Wk, L0_attn_b_Wv, L0_attn_b_Wo, L0_attn_b_lambda_q1, L0_attn_b_lambda_k1, L0_attn_b_lambda_q2, L0_attn_b_lambda_k2, L0_attn_b_subln_weight)
    x = x + _L0_ffn_ref(_layernorm(x, axis=-1), L0_ffn_Wg, L0_ffn_W1, L0_ffn_W3, L0_ffn_W2, L0_ffn_Ws1, L0_ffn_Ws3, L0_ffn_Ws2)
    return x

_drawn_inputs = setup_inputs


def setup_inputs(seed=0):
    import zlib

    import numpy as np

    out = dict(_drawn_inputs(seed))
    spreads = {'L0_attn_b_subln_weight': (1.0, 0.6)}
    factors = {'L0_attn_a_bq': 8.0,
     'L0_attn_a_bk': 8.0,
     'L0_attn_a_bv': 4.888,
     'L0_attn_a_bo': 5.628,
     'L0_attn_b_lambda_q1': 8.0,
     'L0_attn_b_lambda_k1': 8.0,
     'L0_attn_b_lambda_q2': 38.728,
     'L0_attn_b_lambda_k2': 35.0,
     'L0_ffn_Wg': 8.0,
     'L0_ffn_W1': 8.0,
     'L0_ffn_W3': 8.0,
     'L0_ffn_W2': 8.0,
     'L0_ffn_Ws1': 4.104,
     'L0_ffn_Ws3': 3.665,
     'L0_ffn_Ws2': 4.763}
    for name, (base, spread) in spreads.items():
        noise = np.random.default_rng([zlib.crc32(name.encode()), seed]).standard_normal(out[name].shape)
        drawn = base * np.exp(spread * noise) if base else spread * noise
        out[name] = jnp.asarray(drawn.astype(out[name].dtype))
    for name, factor in factors.items():
        out[name] = (out[name] * factor).astype(out[name].dtype)
    return out
```

```python
from contextlib import ExitStack
import math

import numpy as np

import concourse.bass as bass
from concourse import mybir

F32 = mybir.dt.float32
BF16 = mybir.dt.bfloat16
ACT = mybir.ActivationFunctionType
ALU = mybir.AluOpType
X = mybir.AxisListType.X
ds = bass.ds

P = 128
B, T, E = 4, 512, 256
TB = T // P
NT = B * TB
CE = E // P
G = 8
HG = 4
D = 8
W = 64
PR = HG // 2
UNITS = 5
SBANKS = 10
RING = 8
SCALE = float(D) ** -0.5
MASK = -3.0e38
EPS = 1e-5
LAMBDA_INIT = 0.8 - 0.6 * math.exp(-0.3 * 12)
NE, INTER, SHARED = 16, 176, 352
ROWS = NE * INTER
CK = ROWS // P
SCH = [(0, 128), (128, 128), (256, 96)]
M_DMAS = 6 * 16


class Chain:

    def __init__(self, eng, sem, base=0, held=None):
        self.eng, self.sem, self.base, self.n, self.held = eng, sem, base, 0, held

    def __call__(self, ins):
        self.n += 1
        ins.then_inc(self.sem, 1)
        self.eng.wait_ge(self.sem, self.base + self.n)
        if self.held is not None:
            self.eng.sem_inc(self.held, 1)


def build(nc, ins, out, upto=4):
    ctx = ExitStack()
    with ctx:
        def sb(name, shape, dt=F32):
            return ctx.enter_context(nc.sbuf_tensor(name, shape, dt))

        def sem(name):
            return ctx.enter_context(nc.semaphore(name))

        x_sb = sb("x_sb", [P, NT, E])
        y_sb = sb("y_sb", [P, NT, E])
        KW = 32
        o_q, o_k, o_v, o_p = 0, G * NT * 32, 2 * G * NT * 32, 2 * G * NT * 32 + G * NT * 34
        arena = sb("arena", [P, o_p + RING * 1024])
        q_all = arena[:, o_q:o_k].rearrange("p (g t c) -> p g t c", g=G, t=NT)
        k_all = arena[:, o_k:o_v].rearrange("p (g t c) -> p g t c", g=G, t=NT)
        v_all = arena[:, o_v:o_p].rearrange("p (g t c) -> p g t c", g=G, t=NT)
        p_ring = arena[:, o_p:o_p + RING * 1024].rearrange("p (r c) -> p r c", r=RING)
        w13 = arena[:, 0:2 * CE * ROWS].rearrange("p (a c r) -> p a c r", a=2, c=CE)
        arena2 = sb("arena2", [P, 2 * 16 * T // 2])
        qT = arena2[:, 0:16 * T // 2].bitcast(BF16).rearrange("p (r t) -> p r t", r=16)
        kT = arena2[:, 16 * T // 2:].bitcast(BF16).rearrange("p (r t) -> p r t", r=16)
        w2 = arena2[:, 0:CK * E].rearrange("p (c e) -> p c e", c=CK)
        o2 = CK * E
        ws2 = arena2[:, o2:o2 + 3 * E].rearrange("p (c e) -> p c e", c=3)
        o2 += 3 * E
        ws13 = arena2[:, o2:o2 + 2 * CE * SHARED].rearrange("p (a c r) -> p a c r", a=2, c=CE)
        assert o2 + 2 * CE * SHARED <= 16 * T
        stq = sb("stq", [P, 2, 16, W], BF16)
        stk = sb("stk", [P, 2, 16, W], BF16)
        rq = sb("rq", [P, 2, 16, D])
        rk = sb("rk", [P, 2, 16, D])
        v_b = sb("v_b", [P, G, TB, 34])
        oT_sb = sb("oT_sb", [P, T])
        bm3 = sb("bm3", [P, 16, 4])
        bm2 = sb("bm2", [P, 16, 4])
        bm1 = sb("bm1", [P, 16, 2])
        nm = sb("nm", [P, TB, 16])
        nr = sb("nr", [P, 2, TB, 16])
        ms = sb("ms", [P, TB, 3, 16], BF16)
        mT = sb("mT", [48, T], BF16)
        rec = sb("rec", [P, 2, 16])
        otmp = sb("otmp", [P, 16, 16])
        osq = sb("osq", [P, TB, 32])
        ss = sb("ss", [P, NT, 16])
        lam = sb("lam", [P, 8])
        lamv = sb("lamv", [P, 4, D])
        coef = sb("coef", [P, 16])
        mv = sb("mv", [P, NT, 2])
        bst = sb("bst", [P, 2, 6])
        rstd = sb("rstd", [P, NT])
        nw = sb("nw", [P, 4, NT])
        xn = sb("xn", [P, 2, E])
        xnT = sb("xnT", [P, CE, T])
        raw = sb("raw", [P, 320])
        tc = sb("tc", [P, 40, D])
        tsn = sb("tsn", [P, 40, D])
        c_f = sb("c_f", [P, 128 + 2 * TB * D + 16 + 256 + 1])
        c_b = sb("c_b", [P, 128 + 256 + 256], BF16)
        selc = sb("selc", [48, CK, P], BF16)
        wqkv = sb("wqkv", [P, CE, 768])
        wo = sb("wo", [P, CE, E])
        bqkv = sb("bqkv", [P, 384])
        bo = sb("bo", [P, E])
        gsub = sb("gsub", [P, 16])
        wg = sb("wg", [P, CE, NE])
        y_flat = y_sb[:, :, :].rearrange("p t e -> p (t e)")
        sil = y_flat[:, 0:2 * T].rearrange("p (a t) -> p a t", a=2)
        hw = y_flat[:, 2 * T:4 * T].rearrange("p (a t) -> p a t", a=2)
        r16 = y_flat[:, 4 * T:8 * T].rearrange("p (a t i j) -> p a t i j", a=2, t=TB, i=NE)
        sc = sb("sc", [P, TB, NE])
        sx = sb("sx", [P, TB, NE])
        s1 = sb("s1", [P, 4, TB])
        gm = sb("gm", [P, TB, 4])
        g4 = sb("g4", [P, 2, TB, 4, 4])
        g1 = sb("g1", [P, 3, TB, 4])
        cs = sb("cs", [P, TB, 3, NE], BF16)
        cr = sb("cr", [P, 2, TB, NE])
        cT = sb("cT", [48, T], BF16)

        st_ps = ctx.enter_context(nc.psum_tensor("st_ps", [P, 2, 1024], F32))
        s_ps = ctx.enter_context(nc.psum_tensor("s_ps", [P, 2, 512], F32))
        o_ps = ctx.enter_context(nc.psum_tensor("o_ps", [P, 512], F32))
        t_ps = ctx.enter_context(nc.psum_tensor("t_ps", [P, 512], F32))
        t_bf = t_ps[:, :].bitcast(BF16)

        ident_f = c_f[:, 0:128]
        cosT = c_f[:, 128:128 + TB * D].rearrange("p (t d) -> p t d", t=TB)
        sinT = c_f[:, 128 + TB * D:128 + 2 * TB * D].rearrange("p (t d) -> p t d", t=TB)
        o = 128 + 2 * TB * D
        low4 = c_f[:, o:o + 16]
        low16 = c_f[:, o + 16:o + 272]
        epsc = c_f[:, o + 272:o + 273]
        ident_b = c_b[:, 0:128]
        mask_s = c_b[:, 128:384]
        mask_t = c_b[:, 384:640]

        S = {}

        def sm(name):
            if name not in S:
                S[name] = sem(name)
            return S[name]

        def hold(eng, name, value):
            eng.wait_ge(sm(name), value)
            eng.sem_inc(sm("passed"), 1)

        block = ctx.enter_context(nc.Block())
        x_d = ins["x"].rearrange("b (t p) e -> p (b t) e", p=P)
        out_d = out.rearrange("b (t p) e -> p (b t) e", p=P)

        def sp_attn_weights(sp, s):
            n = s + "_w"
            if s == "a":
                sp.dma_start(wqkv[:, :, 0:384], ins["a_wqkv"].rearrange("(c p) n -> p c n", p=P)).then_inc(sm(n), 16)
                sp.dma_start(wo[:], ins["a_wo"].rearrange("(c p) n -> p c n", p=P)).then_inc(sm(n), 16)
                sp.dma_start(bqkv[:], ins["a_bqkv"].partition_broadcast(P)).then_inc(sm(n), 16)
                sp.dma_start(bo[:], ins["a_bo"].partition_broadcast(P)).then_inc(sm(n), 16)
            else:
                sp.dma_start(wqkv[:], ins["b_wqkv"].rearrange("(c p) n -> p c n", p=P)).then_inc(sm(n), 16)
                sp.dma_start(gsub[:], ins["b_g"].partition_broadcast(P)).then_inc(sm(n), 16)
                for j, l in enumerate(("lq1", "lk1", "lq2", "lk2")):
                    sp.dma_start(lamv[:, j, :], ins["b_" + l].partition_broadcast(P)).then_inc(sm(n), 16)

        def sp_move_maxima(sp, s):
            with sp.Fori(0, B) as b:
                for half in range(2):
                    hp = 2 * b + half
                    sp.wait_ge(sm(s + "_m_evac"), hp + 1)
                    for c in range(3):
                        for par in range(2):
                            r = 64 * par + 48 + c
                            sp.dma_start(qT[r:r + 1, 8 * half:8 * half + 8, :],
                                         mT[c * 16 + par * 8:c * 16 + par * 8 + 8, :])\
                              .then_inc(sm(s + "_m_rows"), 16)

        def sp_ffn_weights(sp, f, attn):
            sp.wait_ge(sm(attn + "_norm_done"), 1 + B * G)
            n = f + "_w"
            sp.dma_start(w13[:, 0], ins["w1"].rearrange("(c p) n -> p c n", p=P)).then_inc(sm(n), 16)
            sp.dma_start(w13[:, 1], ins["w3"].rearrange("(c p) n -> p c n", p=P)).then_inc(sm(n), 16)
            sp.dma_start(w2, ins["w2"].rearrange("(c p) n -> p c n", p=P)).then_inc(sm(n), 16)
            sp.dma_start(ws13[:, 0], ins["ws1"].rearrange("(c p) n -> p c n", p=P)).then_inc(sm(n), 16)
            sp.dma_start(ws13[:, 1], ins["ws3"].rearrange("(c p) n -> p c n", p=P)).then_inc(sm(n), 16)
            sp.dma_start(ws2[:, 0:2], ins["ws2"][0:256, :].rearrange("(c p) n -> p c n", p=P)).then_inc(sm(n), 16)
            sp.dma_start(ws2[0:96, 2], ins["ws2"][256:352, :]).then_inc(sm(n), 16)

        @block.sync
        def _(sp):
            for i in range(B):
                sp.dma_start(x_sb[:, 4 * i:4 * i + 4, :], x_d[:, 4 * i:4 * i + 4, :]).then_inc(sm(f"x_in{i}"), 16)
            sp.dma_start(c_f[:], ins["c_f"]).then_inc(sm("consts"), 16)
            sp.dma_start(y_flat[:, 0:640], ins["c_b"]).then_inc(sm("to_cast"), 16)
            sp.dma_start(y_flat[0:48, 640:640 + ROWS], ins["selc"]).then_inc(sm("to_cast"), 16)
            sp_attn_weights(sp, "a")
            sp.dma_start(wg[:], ins["wg"].rearrange("(c p) n -> p c n", p=P)).then_inc(sm("g_w"), 16)
            sp_move_maxima(sp, "a")
            if upto >= 2:
                sp_ffn_weights(sp, "f", "a")
            if upto >= 3:
                sp.wait_ge(sm("a_out_x"), NT)
                sp_attn_weights(sp, "b")
                sp.dma_start(wo[:], ins["b_wo"].rearrange("(c p) n -> p c n", p=P)).then_inc(sm("b_w"), 16)
                sp_move_maxima(sp, "b")
            if upto >= 4:
                sp_ffn_weights(sp, "h", "b")
            last = ["", "a_out_x", "f_x", "b_out_x", "h_x"][upto]
            with sp.Fori(0, B) as b:
                sp.wait_ge(sm(last), (b + 1) * TB)
                sp.dma_start(out_d[:, ds(b * TB, TB), :], x_sb[:, ds(b * TB, TB), :]).then_inc(sm("stored"), 16)
            sp.wait_ge(sm("stored"), 16 * B)

        def pool_split(pool, s, t, g, b, wait_stack, wait_v):
            ch = Chain(pool, sm(s + "_split_chain"), t * (5 if s == "b" else 6), sm("passed"))
            par = g % 2
            q = q_all[:, g, ds(b * TB, TB), :].rearrange("p t (h d) -> p (t h) d", d=D)
            if wait_stack:
                hold(pool, s + "_tr_done", 2 * t - 3)
            st = stq[:, par]
            ch(pool.tensor_copy(st[:, :, 0:24].rearrange("p n (a d) -> p n a d", a=3),
                                q.unsqueeze(2).to_broadcast([P, 16, 3, D])))
            ch(pool.tensor_tensor(rq[:, 0], q, st[:, :, 0:8], ALU.subtract))
            pool.tensor_copy(st[:, :, 24:40].rearrange("p n (a d) -> p n a d", a=2),
                             rq[:, 0].unsqueeze(2).to_broadcast([P, 16, 2, D])).then_inc(sm(s + "_splq"), 1)
            hold(pool, s + "_splq", t + 1)
            ch(pool.tensor_tensor(rq[:, 1], rq[:, 0], st[:, :, 24:32], ALU.subtract))
            pool.tensor_copy(st[:, :, 40:48], rq[:, 1]).then_inc(sm(s + "_split_done"), 1)
            n = 16 if s == "b" else TB
            if s == "b":
                k = k_all[:, g, ds(b * TB, TB), :].rearrange("p t (h d) -> p (t h) d", d=D)
                st = stk[:, par]
            else:
                k = k_all[:, g, ds(b * TB, TB), 0:D]
                st = stk[:, par].rearrange("p (t u) w -> p t u w", u=4)[:, :, 0, :]
            if wait_stack:
                hold(pool, s + "_tr_done", 2 * t - 2)
            kr = rk[:, :, 0:n, :]
            two = st[:, :, 0:48].rearrange("p n (a c) -> p n a c", a=2)
            pool.tensor_copy(two[:, :, :, 0:8], k.unsqueeze(2).to_broadcast([P, n, 2, D])).then_inc(sm(s + "_splk"), 1)
            hold(pool, s + "_splk", 2 * t + 1)
            ch(pool.tensor_tensor(kr[:, 0], k, st[:, :, 0:8], ALU.subtract))
            pool.tensor_copy(st[:, :, 40:48], k)
            pool.tensor_copy(two[:, :, :, 8:16], kr[:, 0].unsqueeze(2).to_broadcast([P, n, 2, D]))\
                .then_inc(sm(s + "_splk"), 1)
            hold(pool, s + "_splk", 2 * t + 2)
            ch(pool.tensor_tensor(kr[:, 1], kr[:, 0], st[:, :, 8:16], ALU.subtract))
            last = pool.tensor_copy(st[:, :, 16:24], kr[:, 1])
            if s == "a":
                ch(last)
                last = pool.tensor_copy(stk[:, par].rearrange("p (t u) w -> p t u w", u=4)[:, :, 1, 0:48],
                                        st[:, :, 0:48])
            last.then_inc(sm(s + "_split_done"), 1)
            hold(pool, s + "_split_done", 2 * t + 2)
            vw = 34 if s == "b" else 9
            if wait_v:
                hold(pool, s + "_p_free", 5 * t - 27)
            pool.tensor_copy(v_b[:, g, :, 0:vw], v_all[:, g, ds(b * TB, TB), 0:vw]).then_inc(sm(s + "_v_done"), 1)

        def pool_attn(pool, s):
            if s == "a":
                pool.wait_ge(sm("a_proj_done"), NT)
            else:
                pool.wait_ge(sm("b_ps_free"), 2 + NT)
            for g in range(G):
                pool_split(pool, s, g, g, 0, g >= 2, False)
            with pool.Fori(0, B - 1) as b:
                for g in range(G):
                    pool_split(pool, s, 8 * b + g + 8, g, b + 1, True, True)

        @block.gpsimd
        def _(pool):
            pool.memset(stq[:, :, :, 48:64], 0.0).then_inc(sm("st_init"), 1)
            pool.memset(stk[:, :, :, 51:64], 0.0).then_inc(sm("st_init"), 1)
            pool.memset(stk[:, :, :, 48:51], 1.0).then_inc(sm("st_init"), 1)
            pool.memset(v_all[:, :, :, D:D + 1], 1.0).then_inc(sm("a_ones"), 1)
            pool.wait_ge(sm("st_init"), 3)
            pool.wait_ge(sm("a_ones"), 1)
            pool_attn(pool, "a")
            if upto >= 3:
                pool.wait_ge(sm("f_x"), NT)
                vo = v_all.rearrange("p g t (h c) -> p g t h c", h=2)
                pool.memset(vo[:, :, :, :, 16:17], 1.0).then_inc(sm("b_ones"), 1)
                pool.wait_ge(sm("b_ones"), 1)
                pool_attn(pool, "b")

        def act_sqrt(act, s):
            act.wait_ge(sm(s + "_var"), 1)
            act.activation(nw[:, 0, :], nw[:, 1, :], ACT.Sqrt).then_inc(sm(s + "_std"), 1)

        def act_tile_T(act, s, t, u):
            src = t_ps if u % 2 == 0 else o_ps
            act.wait_ge(sm(s + "_xt"), t + 1)
            act.activation(xnT[:, :, u * P:(u + 1) * P], src[:, 0:256].rearrange("p (c t) -> p c t", c=CE),
                           ACT.Copy).then_inc(sm(s + "_xnT"), 1)

        def act_proj(act, s):
            act_sqrt(act, s)
            with act.Fori(0, B) as b:
                for u in range(TB):
                    t = TB * b + u
                    act_tile_T(act, s, t, u)
                    if s == "b":
                        act.wait_ge(sm("b_qkv"), 2 * t + 1)
                        act.activation(q_all[:, :, ds(t, 1), :].rearrange("p g t c -> p (g t) c"),
                                       st_ps[:, u % 2, 0:256].rearrange("p (g c) -> p g c", g=G),
                                       ACT.Copy).then_inc(sm("b_q_copied"), 1)

        def act_slot(act, s, n, g, t):
            for u in range(UNITS):
                U = 5 * n + u
                act.wait_ge(sm(s + "_st_done"), U + 1)
                act.wait_ge(sm(s + "_p_free"), U + 1)
                r = (5 * g + u) % RING
                act.activation(p_ring[:, r, :], st_ps[:, (5 * g + u) % 2, :], ACT.Exp, scale=SCALE)\
                    .then_inc(sm(s + "_exp_done"), 1)
            if t is not None:
                act_q_evac(act, s, t, g)
            act.wait_ge(sm(s + "_p_free"), RING + 5 * n + 5)
            act.activation(oT_sb[:], o_ps[:], ACT.Copy).then_inc(sm(s + "_ot_evac"), 1)

        def act_q_evac(act, s, t, g):
            act.wait_ge(sm(s + "_tr_done"), 2 * t + 1)
            act.activation(qT[:, 2 * g:2 * g + 2, :], t_bf.rearrange("p (r t) -> p r t", r=2), ACT.Copy)\
                .then_inc(sm(s + "_q_evac"), 1)

        def act_attn(act, s):
            act.sem_inc(sm(s + "_exp_done"), 2)
            if s == "b":
                act.wait_ge(sm("b_lam"), 1)
                act.activation(lam[:, 2:4], lam[:, 0:2], ACT.Exp).then_inc(sm("b_lam_exp"), 1)
            for g in range(G):
                act_q_evac(act, s, g, g)
            with act.Fori(0, B - 1) as b:
                for g in range(G):
                    act_slot(act, s, 8 * b + g, g, 8 * b + g + 8)
            for g in range(G):
                act_slot(act, s, 8 * (B - 1) + g, g, None)

        def act_out(act, s):
            if s == "b":
                act.wait_ge(sm("b_ms"), 1)
                act.activation(ss[:], ss[:], ACT.Sqrt).then_inc(sm("b_ms_std"), 1)
            with act.Fori(0, NT // 2) as i:
                for u in range(2):
                    t = 2 * i + u
                    src = (t_ps if u == 0 else o_ps)
                    act.wait_ge(sm(s + "_yt"), t + 1)
                    act.activation(xnT[:, :, u * P:(u + 1) * P], src[:, 0:256].rearrange("p (c t) -> p c t", c=CE),
                                   ACT.Copy).then_inc(sm(s + "_yT"), 1)

        def act_ffn(act, f):
            act_sqrt(act, f)
            with act.Fori(0, B) as b:
                for u in range(TB):
                    act_tile_T(act, f, TB * b + u, u)
                act.wait_ge(sm(f + "_sx"), b + 1)
                act.activation(sc[:], sx[:], ACT.Exp).then_inc(sm(f + "_sexp"), 1)
                for c in range(CK + 3):
                    k = (CK + 3) * b + c
                    act.wait_ge(sm(f + "_h"), k + 1)
                    act.wait_ge(sm(f + "_sil_free"), k + 1)
                    m = P if c < CK + 2 else 96
                    act.activation(sil[0:m, c % 2, :], st_ps[0:m, c % 2, 0:512], ACT.Silu).then_inc(sm(f + "_sil"), 1)

        @block.scalar
        def _(act):
            act_proj(act, "a")
            act_attn(act, "a")
            act_out(act, "a")
            if upto >= 2:
                act_ffn(act, "f")
            if upto >= 3:
                act_proj(act, "b")
                act_attn(act, "b")
                act_out(act, "b")
            if upto >= 4:
                act_ffn(act, "h")

        def dve_stats(dve, s, t, last):
            ch = Chain(dve, sm(s + "_st_chain"), 2 * t, sm("passed"))
            xt = x_sb[:, ds(t, 1), :].rearrange("p a e -> p (a e)")
            ch(dve.bn_stats(bst[:, 0, :], xt))
            ch(dve.bn_aggr(bst[:, 1, 0:2], bst[:, 0, :]))
            dve.tensor_copy(mv[:, ds(t, 1), :].rearrange("p a e -> p (a e)"), bst[:, 1, 0:2])\
                .then_inc(sm(s + "_stats"), 1)
            dve.wait_ge(sm(s + "_stats"), t + 1)

        def dve_rstd(dve, s):
            ch = Chain(dve, sm(s + "_rs_chain"))
            dve.tensor_scalar(nw[:, 1, :], mv[:, :, 1], EPS, None, ALU.add).then_inc(sm(s + "_var"), 1)
            dve.wait_ge(sm(s + "_std"), 1)
            ch(dve.reciprocal(nw[:, 2, :], nw[:, 0, :]))
            ch(dve.tensor_tensor(nw[:, 3, :], nw[:, 2, :], nw[:, 2, :], ALU.mult))
            ch(dve.tensor_tensor(nw[:, 3, :], nw[:, 3, :], nw[:, 1, :], ALU.mult))
            ch(dve.tensor_scalar(nw[:, 3, :], nw[:, 3, :], -0.5, 1.5, ALU.mult, ALU.add))
            ch(dve.tensor_tensor(rstd[:], nw[:, 2, :], nw[:, 3, :], ALU.mult))

        def dve_ln(dve, s, t, u):
            dve.tensor_scalar(xn[:, u % 2, :], x_sb[:, ds(t, 1), :].rearrange("p a e -> p (a e)"),
                              mv[:, ds(t, 1), 0:1].rearrange("p a e -> p (a e)"), rstd[:, ds(t, 1)],
                              ALU.subtract, ALU.mult).then_inc(sm(s + "_xn"), 1)

        def dve_proj_tile(dve, s, t, u, ahead):
            ps = st_ps[:, u % 2, :]
            tile = ds(t, 1)
            if s == "a":
                ch = Chain(dve, sm("a_rope"), t * 3)
                dve.wait_ge(sm("a_qkv"), t + 1)
                ch(dve.tensor_tensor(raw[:], ps[:, 0:320], bqkv[:, 0:320], ALU.add))
                dve.tensor_tensor(v_all[:, :, tile, 0:D].rearrange("p g t c -> p (g t) c"),
                                  ps[:, 320:384].rearrange("p (g c) -> p g c", g=G),
                                  bqkv[:, 320:384].rearrange("p (g c) -> p g c", g=G), ALU.add)\
                    .then_inc(sm("a_ps_free"), 1)
                if ahead:
                    dve_ln(dve, s, t + 2, u)
                r3 = raw[:].rearrange("p (h d) -> p h d", d=D)
                ch(dve.tensor_tensor(tc[:], r3, cosT[:, u:u + 1, :].to_broadcast([P, 40, D]), ALU.mult))
                ch(dve.tensor_tensor(tsn[:], r3, sinT[:, u:u + 1, :].to_broadcast([P, 40, D]), ALU.mult))
                for lo in range(2):
                    a, c = 4 * lo, 4 - 4 * lo
                    qo = q_all[:, :, tile, :].rearrange("p g t (h d) -> p (g t) h d", d=D)
                    dve.tensor_tensor(qo[:, :, :, a:a + 4],
                                      tc[:, 0:32, a:a + 4].rearrange("p (g h) d -> p g h d", g=G),
                                      tsn[:, 0:32, c:c + 4].rearrange("p (g h) d -> p g h d", g=G), ALU.add)
                    last = dve.tensor_tensor(k_all[:, :, tile, a:a + 4].rearrange("p g t c -> p (g t) c"),
                                             tc[:, 32:40, a:a + 4], tsn[:, 32:40, c:c + 4], ALU.add)
                last.then_inc(sm("a_proj_done"), 1)
                dve.wait_ge(sm("a_proj_done"), t + 1)
            else:
                dve.wait_ge(sm("b_qkv"), 2 * t + 1)
                dve.wait_ge(sm("b_q_copied"), t + 1)
                dve.tensor_copy(k_all[:, :, tile, :].rearrange("p g t c -> p (g t) c"),
                                ps[:, 256:512].rearrange("p (g c) -> p g c", g=G))
                if ahead:
                    dve_ln(dve, s, t + 2, u)
                dve.wait_ge(sm("b_qkv"), 2 * t + 2)
                for h in range(2):
                    last = dve.tensor_copy(v_all[:, :, tile, 17 * h:17 * h + 16].rearrange("p g t c -> p (g t) c"),
                                           ps[:, 512:768].rearrange("p (g h c) -> p g h c", g=G, h=2)[:, :, h, :])
                last.then_inc(sm("b_ps_free"), 1)

        def dve_proj(dve, s):
            dve_rstd(dve, s)
            dve.wait_ge(sm("consts"), 16)
            dve.wait_ge(sm(s + "_w"), 64 if s == "a" else 112)
            dve_ln(dve, s, 0, 0)
            dve_ln(dve, s, 1, 1)
            with dve.Fori(0, B - 1) as b:
                for u in range(TB):
                    dve_proj_tile(dve, s, TB * b + u, u, True)
            for u in range(TB):
                dve_proj_tile(dve, s, TB * (B - 1) + u, u, u < 2)

        def dve_max(dve, s, n, g, k):
            h0 = HG * (g % 4)
            if k < 4:
                dst = bm3[:, h0 + k, :]
            elif k < 8:
                dst = bm2[:, h0 + k - 4, :]
            else:
                dst = bm1[:, h0:h0 + 4, :].rearrange("p (j a) c -> p a j c", a=2)[:, k - 8]
            dve.wait_ge(sm(s + "_s_done"), 10 * n + k + 1)
            src = s_ps[:, k % 2, :]
            src = src.rearrange("p (c k) -> p c k", c=4) if k < 8 else src.rearrange("p (j c k) -> p j c k", j=2, c=2)
            dve.tensor_reduce(dst, src, X, ALU.max)\
                .then_inc(sm(s + "_max_done"), 1)

        def dve_maxima(dve, s, hp):
            ch = Chain(dve, sm(s + "_m_chain"), hp * 8)

            def to(i):
                return nm[:, i, :].rearrange("p (par pr) -> p pr par", par=2)

            dve.wait_ge(sm(s + "_max_done"), (4 * hp + 4) * 10 + 2)
            ch(dve.tensor_reduce(to(3), bm3[:].rearrange("p (pr par) k -> p pr par k", par=2), X, ALU.max, negate=True))
            ch(dve.tensor_reduce(to(2), bm2[:, :, 0:3].rearrange("p (pr par) k -> p pr par k", par=2), X, ALU.max,
                                 negate=True))
            ch(dve.tensor_reduce(to(1), bm1[:].rearrange("p (pr par) k -> p pr par k", par=2), X, ALU.max, negate=True))
            ch(dve.tensor_scalar(to(0), bm2[:, :, 3].rearrange("p (pr par) -> p pr par", par=2), -1.0, None, ALU.mult))
            ch(dve.tensor_copy(ms[:, :, 0, :], nm[:]))
            ch(dve.tensor_tensor(nr[:, 0], nm[:], ms[:, :, 0, :], ALU.subtract))
            ch(dve.tensor_copy(ms[:, :, 1, :], nr[:, 0]))
            ch(dve.tensor_tensor(nr[:, 1], nr[:, 0], ms[:, :, 1, :], ALU.subtract))
            dve.tensor_copy(ms[:, :, 2, :], nr[:, 1]).then_inc(sm(s + "_m_split"), 1)

        def dve_m_evac(dve, s, hp, first=False):
            dve.wait_ge(sm(s + "_m_tr"), hp + 1)
            if not first:
                dve.wait_ge(sm(s + "_m_rows"), M_DMAS * hp)
            dve.tensor_copy(mT[:], t_bf[0:48, 0:T]).then_inc(sm(s + "_m_evac"), 1)

        def dve_k_evac(dve, s, t, g):
            dve.wait_ge(sm(s + "_tr_done"), 2 * t + 2)
            if s == "b":
                dve.tensor_copy(kT[:, 2 * g:2 * g + 2, :], t_bf.rearrange("p (r t) -> p r t", r=2))\
                    .then_inc(sm(s + "_k_evac"), 1)
            else:
                dve.tensor_copy(kT[:, g, :], t_bf[:, 0:T]).then_inc(sm(s + "_k_evac"), 1)

        def dve_norm(dve, s, n, g, b):
            o3 = t_ps[:, :].rearrange("p (n c) -> p n c", c=32)
            dve.wait_ge(sm(s + "_otr_done"), n + 1)
            tiles = ds(b * TB, TB)
            if s == "a":
                ch = Chain(dve, sm("a_norm_chain"), n)
                ch(dve.reciprocal(rec[:, 0, :], o3[:, :, D]))
                dve.tensor_tensor(y_sb[:, tiles, 32 * g:32 * g + 32].rearrange("p t (h d) -> p t h d", d=D),
                                  o3[:, :, 0:D].rearrange("p (t h) d -> p t h d", t=TB),
                                  rec[:, 0, :].rearrange("p (t h) -> p t h", t=TB).unsqueeze(3).to_broadcast([P, TB, HG, D]),
                                  ALU.mult).then_inc(sm("a_norm_done"), 1)
                dve.wait_ge(sm("a_norm_done"), n + 2)
            else:
                ch = Chain(dve, sm("b_norm_chain"), n * 5)
                ch(dve.reciprocal(rec[:, 0, :], o3[:, :, 16]))
                ch(dve.tensor_tensor(rec[:, 1, :], rec[:, 0, :], coef[:], ALU.mult))
                dve.tensor_tensor(otmp[:], o3[:, :, 0:16], rec[:, 1, :].unsqueeze(2).to_broadcast([P, 16, 16]),
                                  ALU.mult).then_inc(sm("b_norm_done"), 1)
                dve.wait_ge(sm("b_norm_done"), n + 2)
                o5 = otmp[:].rearrange("p (t h a) c -> p t h a c", t=TB, a=2)
                yv = y_sb[:, tiles, 32 * g:32 * g + 32]
                ch(dve.tensor_tensor(yv.rearrange("p t (h c) -> p t h c", h=2), o5[:, :, :, 0, :], o5[:, :, :, 1, :],
                                     ALU.add))
                ch(dve.tensor_tensor(osq[:], yv, yv, ALU.mult))
                ch(dve.tensor_reduce(ss[:, tiles, 2 * g:2 * g + 2], osq[:].rearrange("p t (h c) -> p t h c", h=2),
                                     X, ALU.add))

        def dve_slot(dve, s, n, g, b, with_s, with_t):
            sn, sg = n + 7, (g - 1) % G
            if g == 1:
                dve_m_evac(dve, s, 2 * b + 1)
            if g == 5 and with_t:
                dve_m_evac(dve, s, 2 * b + 2)
            if with_s:
                for k in range(7):
                    dve_max(dve, s, sn, sg, k)
            if with_t:
                dve_k_evac(dve, s, n + 8, g)
            if with_s:
                for k in range(7, SBANKS):
                    dve_max(dve, s, sn, sg, k)
            dve_norm(dve, s, n, g, b)
            if with_s and sg == 3:
                dve_maxima(dve, s, 2 * b + 2)
            if with_s and sg == 7:
                dve_maxima(dve, s, 2 * b + 1)

        def dve_attn(dve, s):
            dve.sem_inc(sm(s + "_max_done"), 2)
            dve.sem_inc(sm(s + "_norm_done"), 1)
            dve.memset(o_ps[:], 0.0).then_inc(sm(s + "_o_init"), 1)
            if s == "b":
                ch = Chain(dve, sm("b_lam_chain"))
                ch(dve.tensor_tensor(lamv[:, 0, :], lamv[:, 0, :], lamv[:, 1, :], ALU.mult))
                ch(dve.tensor_tensor(lamv[:, 2, :], lamv[:, 2, :], lamv[:, 3, :], ALU.mult))
                dve.tensor_reduce(lam[:, 0:2], lamv[:].rearrange("p (a c) d -> p a c d", c=2)[:, :, 0, :], X, ALU.add)\
                    .then_inc(sm("b_lam"), 1)
                dve.wait_ge(sm("b_lam_exp"), 1)
                ch(dve.tensor_tensor(lam[:, 4:5], lam[:, 3:4], lam[:, 2:3], ALU.subtract))
                ch(dve.tensor_scalar(lam[:, 5:6], lam[:, 4:5], -LAMBDA_INIT, None, ALU.add))
                ch(dve.memset(coef[:], 1.0))
                cv = coef[:].rearrange("p (n a) -> p n a", a=2)
                ch(dve.tensor_scalar(cv[:, :, 1], cv[:, :, 1], lam[:, 5:6], None, ALU.mult))
            dve_k_evac(dve, s, 0, 0)
            for g in range(G - 1):
                if g == 4:
                    dve_m_evac(dve, s, 0, first=True)
                for k in range(SBANKS):
                    dve_max(dve, s, g, g, k)
                if g == 3:
                    dve_maxima(dve, s, 0)
                dve_k_evac(dve, s, g + 1, g + 1)
            with dve.Fori(0, B - 1) as b:
                for g in range(G):
                    dve_slot(dve, s, 8 * b + g, g, b, True, True)
            for g in range(G):
                dve_slot(dve, s, 8 * (B - 1) + g, g, B - 1, g == 0, False)

        def dve_out(dve, s):
            if s == "b":
                ch = Chain(dve, sm("b_ms_chain"))
                dve.wait_ge(sm("b_norm_chain"), 5 * B * G)
                dve.tensor_scalar(ss[:], ss[:], 1.0 / 16, EPS, ALU.mult, ALU.add).then_inc(sm("b_ms"), 1)
                dve.wait_ge(sm("b_ms_std"), 1)
                ch(dve.reciprocal(ss[:], ss[:]))
                ch(dve.tensor_scalar(gsub[:], gsub[:], 1.0 - LAMBDA_INIT, None, ALU.mult))
            with dve.Fori(0, NT // 2) as i:
                for u in range(2):
                    t = 2 * i + u
                    yt = y_sb[:, ds(t, 1), :].rearrange("p a e -> p (a e)")
                    if s == "a":
                        dve.tensor_copy(xn[:, u, :], yt).then_inc(sm("a_y"), 1)
                    else:
                        yv = yt.rearrange("p (h c) -> p h c", h=16)
                        xv = xn[:, u, :].rearrange("p (h c) -> p h c", h=16)
                        r = ss[:, ds(t, 1), :].rearrange("p a h -> p (a h)").unsqueeze(2).to_broadcast([P, 16, 16])
                        ch = Chain(dve, sm("b_y_chain"), t)
                        ch(dve.tensor_tensor(xv, yv, r, ALU.mult))
                        dve.tensor_tensor(xv, xv, gsub[:].unsqueeze(1).to_broadcast([P, 16, 16]), ALU.mult)\
                            .then_inc(sm("b_y"), 1)
                for u in range(2):
                    t = 2 * i + u
                    xt = x_sb[:, ds(t, 1), :].rearrange("p a e -> p (a e)")
                    dve.wait_ge(sm(s + "_po"), t + 1)
                    if s == "a":
                        ch = Chain(dve, sm("a_bo_chain"), t)
                        ch(dve.tensor_tensor(xt, xt, bo[:], ALU.add))
                    dve.tensor_tensor(xt, xt, st_ps[:, u, 0:E], ALU.add).then_inc(sm(s + "_out_x"), 1)
                    hold(dve, s + "_out_x", t + 1)
                    dve_stats(dve, s + "o", t, False)

        def dve_ffn(dve, f, loads):
            dve_rstd(dve, f)
            dve.wait_ge(sm("g_w"), 16)
            with dve.Fori(0, B) as b:
                for u in range(TB):
                    if u >= 2:
                        dve.wait_ge(sm(f + "_xt"), TB * b + u - 1)
                    dve_ln(dve, f, TB * b + u, u)
                ch = Chain(dve, sm(f + "_r_chain"), b * 19)
                lg = t_ps[:, 256:320].rearrange("p (t e) -> p t e", t=TB)
                dve.wait_ge(sm(f + "_lg"), b + 1)
                ch(dve.tensor_reduce(s1[:, 0, :], lg, X, ALU.max))
                dve.tensor_tensor(sx[:], lg, s1[:, 0, :].unsqueeze(2).to_broadcast([P, TB, NE]), ALU.subtract)\
                    .then_inc(sm(f + "_sx"), 1)
                dve.wait_ge(sm(f + "_sexp"), b + 1)
                ch(dve.tensor_reduce(s1[:, 1, :], sc[:], X, ALU.add))
                ch(dve.reciprocal(s1[:, 2, :], s1[:, 1, :]))
                ch(dve.tensor_tensor(sc[:], sc[:], s1[:, 2, :].unsqueeze(2).to_broadcast([P, TB, NE]), ALU.mult))
                ch(dve.tensor_reduce(gm[:], sc[:].rearrange("p t (g e) -> p t g e", g=4), X, ALU.max))
                gj = gm[:].unsqueeze(2).to_broadcast([P, TB, 4, 4])
                gi = gm[:].unsqueeze(3).to_broadcast([P, TB, 4, 4])
                l4 = low4.rearrange("p (i j) -> p i j", i=4).unsqueeze(1).to_broadcast([P, TB, 4, 4])
                ch(dve.tensor_tensor(g4[:, 0], gj, gi, ALU.is_gt))
                ch(dve.tensor_tensor(g4[:, 1], gj, gi, ALU.is_equal))
                ch(dve.tensor_tensor(g4[:, 1], g4[:, 1], l4, ALU.mult))
                ch(dve.tensor_tensor(g4[:, 0], g4[:, 0], g4[:, 1], ALU.add))
                ch(dve.tensor_reduce(g1[:, 0], g4[:, 0], X, ALU.add))
                ch(dve.tensor_scalar(g1[:, 1], g1[:, 0], 2.0, None, ALU.is_lt))
                ch(dve.tensor_scalar(g1[:, 2], g1[:, 1], -1.0, None, ALU.add))
                sv = sx[:].rearrange("p t (g e) -> p t g e", g=4)
                ch(dve.tensor_tensor(sv, sc[:].rearrange("p t (g e) -> p t g e", g=4),
                                     g1[:, 1].unsqueeze(3).to_broadcast([P, TB, 4, 4]), ALU.mult))
                ch(dve.tensor_tensor(sv, sv, g1[:, 2].unsqueeze(3).to_broadcast([P, TB, 4, 4]), ALU.add))
                for t in range(TB):
                    sj = sx[:, t, :].unsqueeze(1).to_broadcast([P, NE, NE])
                    si = sx[:, t, :].unsqueeze(2).to_broadcast([P, NE, NE])
                    dve.tensor_tensor(r16[:, 0, t], sj, si, ALU.is_gt)
                    ins_ = dve.tensor_tensor(r16[:, 1, t], sj, si, ALU.is_equal)
                ch(ins_)
                l16 = low16.unsqueeze(1).to_broadcast([P, TB, 256])
                f1 = r16[:, 1].rearrange("p t i j -> p t (i j)")
                ch(dve.tensor_tensor(f1, f1, l16, ALU.mult))
                ch(dve.tensor_tensor(r16[:, 0], r16[:, 0], r16[:, 1], ALU.add))
                ch(dve.tensor_reduce(cr[:, 0], r16[:, 0], X, ALU.add))
                ch(dve.scalar_tensor_tensor(cr[:, 1], cr[:, 0], 4.0, sc[:], ALU.is_lt, ALU.mult))
                dve_ffn_parts(dve, f, b)
                for c in range(CK + 3):
                    k = (CK + 3) * b + c
                    m = P if c < CK + 2 else 96
                    dve.wait_ge(sm(f + "_sil"), k + 1)
                    ch = Chain(dve, sm(f + "_hw_chain"), CK * b + c)
                    if c < CK:
                        dve.wait_ge(sm(f + "_h"), k + 1)
                        ch(dve.tensor_tensor(sil[:, c % 2, :], sil[:, c % 2, :], st_ps[:, c % 2, 512:1024], ALU.mult))
                        dve.wait_ge(sm(f + "_hw_used"), k + 1)
                        dve.wait_ge(sm(f + "_cw"), CK * b + c + 1)
                        dve.tensor_tensor(hw[:, c % 2, :], sil[:, c % 2, :], o_ps[:, :], ALU.mult)\
                            .then_inc(sm(f + "_sil_free"), 1)
                    else:
                        dve.wait_ge(sm(f + "_hw_used"), k + 1)
                        dve.tensor_tensor(hw[0:m, c % 2, :], sil[0:m, c % 2, :], st_ps[0:m, c % 2, 512:1024], ALU.mult)\
                            .then_inc(sm(f + "_sil_free"), 1)
                for u in range(TB):
                    t = TB * b + u
                    xt = x_sb[:, ds(t, 1), :].rearrange("p a e -> p (a e)")
                    dve.wait_ge(sm(f + "_hw_used"), (CK + 3) * (b + 1) + 2)
                    dve.tensor_tensor(xt, xt, s_ps[:, u // 2, (u % 2) * E:(u % 2) * E + E], ALU.add)\
                        .then_inc(sm(f + "_x"), 1)
                    hold(dve, f + "_x", t + 1)
                    dve_stats(dve, f + "o", t, False)

        def dve_ffn_parts(dve, f, b):
            ch = Chain(dve, sm(f + "_c_chain"), b * 4)
            ch(dve.tensor_copy(cs[:, :, 0, :], cr[:, 1]))
            ch(dve.tensor_tensor(cr[:, 0], cr[:, 1], cs[:, :, 0, :], ALU.subtract))
            ch(dve.tensor_copy(cs[:, :, 1, :], cr[:, 0]))
            ch(dve.tensor_tensor(cr[:, 1], cr[:, 0], cs[:, :, 1, :], ALU.subtract))
            dve.tensor_copy(cs[:, :, 2, :], cr[:, 1]).then_inc(sm(f + "_cs"), 1)
            dve.wait_ge(sm(f + "_ct"), b + 1)
            dve.tensor_copy(cT[:], t_bf[0:48, 0:T]).then_inc(sm(f + "_cT"), 1)

        @block.vector
        def _(dve):
            dve.wait_ge(sm("to_cast"), 32)
            dve.tensor_copy(c_b[:], y_flat[:, 0:640]).then_inc(sm("cast"), 1)
            dve.tensor_copy(selc[:].rearrange("p c r -> p (c r)"), y_flat[0:48, 640:640 + ROWS])\
                .then_inc(sm("cast"), 1)
            dve.wait_ge(sm("cast"), 2)
            for i in range(B):
                dve.wait_ge(sm(f"x_in{i}"), 16)
                for u in range(TB):
                    dve_stats(dve, "x", TB * i + u, False)
            dve_proj(dve, "a")
            dve_attn(dve, "a")
            dve_out(dve, "a")
            if upto >= 2:
                dve_ffn(dve, "f", None)
            if upto >= 3:
                dve_proj(dve, "b")
                dve_attn(dve, "b")
                dve_out(dve, "b")
            if upto >= 4:
                dve_ffn(dve, "h", None)

        def pe_transpose_tile(pe, s, t, u):
            dst = t_ps if u % 2 == 0 else o_ps
            pe.wait_ge(sm(s + "_xn"), t + 1)
            for c in range(CE):
                last = pe.transpose(dst[:, c * P:(c + 1) * P], xn[:, u % 2, c * P:(c + 1) * P], ident_f)
            return last

        def pe_proj_tile(pe, s, t, u, ahead):
            if ahead:
                pe_transpose_tile(pe, s, t + 1, u + 1).then_inc(sm(s + "_xt"), 1)
            pe.wait_ge(sm(s + "_xnT"), t + 1)
            pe.wait_ge(sm(s + "_ps_free"), t + 1)
            nqk = 384 if s == "a" else 512
            for c in range(CE):
                mm = pe.matmul(st_ps[:, u % 2, 0:nqk], xnT[:, c, u * P:(u + 1) * P], wqkv[:, c, 0:nqk],
                               start=c == 0, stop=c == CE - 1)
            mm.then_inc(sm(s + "_qkv"), 1)
            if s == "b":
                for c in range(CE):
                    mm = pe.matmul(st_ps[:, u % 2, 512:768], xnT[:, c, u * P:(u + 1) * P], wqkv[:, c, 512:768],
                                   start=c == 0, stop=c == CE - 1)
                mm.then_inc(sm(s + "_qkv"), 1)

        def pe_proj(pe, s):
            pe.sem_inc(sm(s + "_ps_free"), 2)
            pe_transpose_tile(pe, s, 0, 0).then_inc(sm(s + "_xt"), 1)
            with pe.Fori(0, B - 1) as b:
                for u in range(TB):
                    pe_proj_tile(pe, s, TB * b + u, u, True)
            for u in range(TB):
                pe_proj_tile(pe, s, TB * (B - 1) + u, u, u < TB - 1)

        def q_of(g, h, a, b_):
            r = 64 * (h % 2)
            return qT[r:r + W, 2 * g + h // 2, a:b_]

        def k_of(s, g, h, a, b_):
            r = 64 * (h % 2)
            return kT[r:r + W, (2 * g + h // 2) if s == "b" else g, a:b_]

        def pe_unit(pe, s, n, g, u):
            buf = (5 * g + u) % 2
            pe.wait_ge(sm(s + "_exp_done"), 5 * n + u + 1)
            for bank in range(2):
                ps = st_ps[:, buf, 512 * bank:512 * bank + 512]
                if u < 2:
                    h = 2 * u + bank
                    pe.matmul(ps, k_of(s, g, h, 0, P), q_of(g, h, 0, T), start=True, stop=False,
                              skip_group_check=True)
                    mm = pe.matmul(ps[:, 0:P], ident_b, mask_t[:, 0:P], start=False, stop=True, skip_group_check=True)
                elif u < 4:
                    h = 2 * (u - 2) + bank
                    pe.matmul(ps[:, 0:P], k_of(s, g, h, 3 * P, 4 * P), q_of(g, h, 3 * P, T), start=True, stop=False,
                              skip_group_check=True)
                    pe.matmul(ps[:, P:T], k_of(s, g, h, P, 2 * P), q_of(g, h, P, T), start=False, stop=False,
                              skip_group_check=True)
                    mm = pe.matmul(ps[:, 0:2 * P], ident_b, mask_t, start=False, stop=True, skip_group_check=True)
                else:
                    for j in range(2):
                        h = 2 * j + bank
                        pe.matmul(ps[:, 256 * j:256 * j + 256], k_of(s, g, h, 2 * P, 3 * P), q_of(g, h, 2 * P, T),
                                  start=j == 0, stop=False, skip_group_check=True)
                    mm = pe.matmul(ps.rearrange("p (j c) -> p j c", j=2)[:, :, 0:P], ident_b,
                                   mask_t.rearrange("p (j c) -> p j c", j=2), start=False, stop=True,
                                   skip_group_check=True)
            mm.then_inc(sm(s + "_st_done"), 1)

        def pe_scores(pe, s, n, g, k):
            ps = s_ps[:, k % 2, :]
            if k == 0:
                pe.wait_ge(sm(s + "_q_evac"), n + 1)
                pe.wait_ge(sm(s + "_k_evac"), n + 1)
            pe.wait_ge(sm(s + "_max_done"), 10 * n + k + 1)
            if k < 4:
                pe.matmul(ps, q_of(g, k, 3 * P, T), k_of(s, g, k, 0, T), start=True, stop=False, skip_group_check=True)
                mm = pe.matmul(ps[:, 3 * P:T], ident_b, mask_s[:, 0:P], start=False, stop=True, skip_group_check=True)
            elif k < 8:
                h = k - 4
                pe.matmul(ps[:, 0:3 * P], q_of(g, h, 2 * P, 3 * P), k_of(s, g, h, 0, 3 * P), start=True, stop=False,
                          skip_group_check=True)
                pe.matmul(ps[:, 3 * P:T], q_of(g, h, 0, P), k_of(s, g, h, 0, P), start=False, stop=False,
                          skip_group_check=True)
                mm = pe.matmul(ps[:, 2 * P:T], ident_b, mask_s, start=False, stop=True, skip_group_check=True)
            else:
                for j in range(2):
                    h = 2 * j + k - 8
                    pe.matmul(ps[:, 256 * j:256 * j + 256], q_of(g, h, P, 2 * P), k_of(s, g, h, 0, 2 * P),
                              start=j == 0, stop=False, skip_group_check=True)
                mm = pe.matmul(ps.rearrange("p (j c) -> p j c", j=2)[:, :, P:2 * P], ident_b,
                               mask_s.rearrange("p (j c) -> p j c", j=2), start=False, stop=True,
                               skip_group_check=True)
            mm.then_inc(sm(s + "_s_done"), 1)

        def pe_tr_q(pe, s, t, g):
            pe.wait_ge(sm(s + "_split_done"), 2 * t + 1)
            for pr in range(PR):
                for i in range(TB):
                    src = stq[:, g % 2, i * HG + 2 * pr:i * HG + 2 * pr + 2, :].rearrange("p h w -> p (h w)")
                    mm = pe.transpose(t_bf[:, pr * T + i * P:pr * T + (i + 1) * P], src, ident_b)
            mm.then_inc(sm(s + "_tr_done"), 1)

        def pe_tr_k(pe, s, t, g):
            pe.wait_ge(sm(s + "_split_done"), 2 * t + 2)
            pe.wait_ge(sm(s + "_q_evac"), t + 1)
            for pr in range(PR if s == "b" else 1):
                for i in range(TB):
                    src = stk[:, g % 2, i * HG + 2 * pr:i * HG + 2 * pr + 2, :].rearrange("p h w -> p (h w)")
                    mm = pe.transpose(t_bf[:, pr * T + i * P:pr * T + (i + 1) * P], src, ident_b)
            mm.then_inc(sm(s + "_tr_done"), 1)

        def pe_m_tr(pe, s, hp):
            hold(pe, s + "_m_split", hp + 1)
            for i in range(TB):
                mm = pe.transpose(t_bf[0:48, i * P:(i + 1) * P], ms[:, i].rearrange("p c h -> p (c h)"), ident_b)
            mm.then_inc(sm(s + "_m_tr"), 1)

        def pe_pv(pe, s, n, g, u, j, last=False):
            vw = 9 if s == "a" else 17
            for h in range(HG):
                v = v_b[:, g, j, 0:9] if s == "a" else v_b[:, g, j, 17 * (h // 2):17 * (h // 2) + 17]
                if j == 0:
                    r, a, c = 5 * g + h // 2, 512 * (h % 2), 512
                elif j == 1:
                    r, a, c = 5 * g + 2 + h // 2, 512 * (h % 2) + P, 384
                elif j == 3:
                    r, a, c = 5 * g + 2 + h // 2, 512 * (h % 2), P
                else:
                    r, a, c = 5 * g + 4, 512 * (h % 2) + 256 * (h // 2), 256
                mm = pe.matmul(o_ps[32 * h:32 * h + vw, T - c:T], v, p_ring[:, r % RING, a:a + c], start=j == 0,
                               stop=last, tile_position=(0, 32 * h), skip_group_check=True)
            return mm

        def pe_slot(pe, s, n, g, b, with_s, with_t):
            sn, sg = n + 7, (g - 1) % G

            def scores(*ks):
                if with_s:
                    for k in ks:
                        pe_scores(pe, s, sn, sg, k)

            if g % 4 == 0:
                pe.wait_ge(sm(s + "_m_rows"), M_DMAS * (2 * b + 1 + g // 4))
            pe_unit(pe, s, n, g, 0)
            pe_unit(pe, s, n, g, 1)
            pe.wait_ge(sm(s + "_norm_done"), n + 1)
            m_now = g == 1 or (g == 5 and with_t)
            if m_now:
                pe_m_tr(pe, s, 2 * b + (1 if g == 1 else 2))
            scores(0, 1)
            pe_unit(pe, s, n, g, 2)
            scores(2, 3)
            pe.wait_ge(sm(s + "_v_done"), n + 1)
            pe.wait_ge(sm(s + "_exp_done"), 5 * n + 4)
            pe_pv(pe, s, n, g, 0, 0).then_inc(sm(s + "_p_free"), 2)
            pe_unit(pe, s, n, g, 3)
            scores(4, 5)
            pe_unit(pe, s, n, g, 4)
            if m_now:
                pe.wait_ge(sm(s + "_m_evac"), 2 * b + (2 if g == 1 else 3))
            if with_t:
                pe_tr_q(pe, s, n + 8, g)
            scores(6)
            pe.wait_ge(sm(s + "_exp_done"), 5 * n + 6)
            pe_pv(pe, s, n, g, 2, 1)
            pe_pv(pe, s, n, g, 2, 3).then_inc(sm(s + "_p_free"), 2)
            if with_t:
                pe_tr_k(pe, s, n + 8, g)
            scores(7, 8)
            pe.wait_ge(sm(s + "_exp_done"), 5 * n + 7)
            pe_pv(pe, s, n, g, 4, 2, last=True).then_inc(sm(s + "_p_free"), 1)
            scores(9)
            if with_t:
                pe.wait_ge(sm(s + "_k_evac"), n + 9)
            pe.wait_ge(sm(s + "_ot_evac"), n + 1)
            for i in range(TB):
                mm = pe.transpose(t_ps[:, i * P:(i + 1) * P], oT_sb[:, i * P:(i + 1) * P], ident_f)
            mm.then_inc(sm(s + "_otr_done"), 1)

        def pe_attn(pe, s):
            pe.sem_inc(sm(s + "_p_free"), RING)
            pe.wait_ge(sm(s + "_o_init"), 1)
            if s == "a":
                pe.wait_ge(sm("cast"), 2)
            pe_tr_q(pe, s, 0, 0)
            pe_tr_k(pe, s, 0, 0)
            for g in range(G - 1):
                pe.wait_ge(sm(s + "_k_evac"), g + 1)
                if g == 4:
                    pe_m_tr(pe, s, 0)
                for k in range(SBANKS):
                    pe_scores(pe, s, g, g, k)
                if g == 4:
                    pe.wait_ge(sm(s + "_m_evac"), 1)
                pe_tr_q(pe, s, g + 1, g + 1)
                pe_tr_k(pe, s, g + 1, g + 1)
            pe.wait_ge(sm(s + "_k_evac"), G)
            with pe.Fori(0, B - 1) as b:
                for g in range(G):
                    pe_slot(pe, s, 8 * b + g, g, b, True, True)
            for g in range(G):
                pe_slot(pe, s, 8 * (B - 1) + g, g, B - 1, g == 0, False)

        def pe_out(pe, s):
            pe.wait_ge(sm(s + "_norm_done"), 1 + B * G)
            with pe.Fori(0, NT // 2) as i:
                for u in range(2):
                    t = 2 * i + u
                    dst = t_ps if u == 0 else o_ps
                    pe.wait_ge(sm(s + "_y"), t + 1)
                    for c in range(CE):
                        mm = pe.transpose(dst[:, c * P:(c + 1) * P], xn[:, u, c * P:(c + 1) * P], ident_f)
                    mm.then_inc(sm(s + "_yt"), 1)
                for u in range(2):
                    t = 2 * i + u
                    pe.wait_ge(sm(s + "_yT"), t + 1)
                    for c in range(CE):
                        mm = pe.matmul(st_ps[:, u, 0:E], xnT[:, c, u * P:(u + 1) * P], wo[:, c, :], start=c == 0,
                                       stop=c == CE - 1)
                    mm.then_inc(sm(s + "_po"), 1)

        def pe_ffn(pe, f):
            pe.sem_inc(sm(f + "_sil_free"), 2)
            pe.sem_inc(sm(f + "_hw_used"), 2)
            pe.wait_ge(sm("g_w"), 16)
            pe.wait_ge(sm(f + "_w"), 7 * 16)
            N = CK + 3
            with pe.Fori(0, B) as b:
                for u in range(TB):
                    t = TB * b + u
                    if u >= 2:
                        pe.wait_ge(sm(f + "_xnT"), t - 1)
                    pe_transpose_tile(pe, f, t, u).then_inc(sm(f + "_xt"), 1)
                pe.wait_ge(sm(f + "_xnT"), TB * b + TB)
                for u in range(TB):
                    for c in range(CE):
                        mm = pe.matmul(t_ps[:, 256 + 16 * u:272 + 16 * u], xnT[:, c, u * P:(u + 1) * P], wg[:, c, :],
                                       start=c == 0, stop=c == CE - 1)
                mm.then_inc(sm(f + "_lg"), 1)

                def inner(c):
                    k = N * b + c
                    m = P if c < CK + 2 else 96
                    pe.wait_ge(sm(f + "_sil_free"), k + 1)
                    for a in range(2):
                        for e in range(CE):
                            if c < CK:
                                wl = w13[:, a, e, c * P:(c + 1) * P]
                            else:
                                wl = ws13[:, a, e, (c - CK) * P:(c - CK) * P + m]
                            mm = pe.matmul(st_ps[0:m, c % 2, 512 * a:512 * a + 512], wl, xnT[:, e, :],
                                           start=e == 0, stop=e == CE - 1)
                    mm.then_inc(sm(f + "_h"), 1)

                def weights(c):
                    pe.wait_ge(sm(f + "_sil_free"), N * b + c + 2)
                    pe.matmul(o_ps[:], selc[:, c, :], cT[:], start=True, stop=True).then_inc(sm(f + "_cw"), 1)

                def outer(c):
                    k = N * b + c
                    m = P if c < CK + 2 else 96
                    pe.wait_ge(sm(f + "_sil_free"), k + 3)
                    w = w2[:, c, :] if c < CK else ws2[0:m, c - CK, :]
                    for u in range(TB):
                        mm = pe.matmul(s_ps[:, u // 2, (u % 2) * E:(u % 2) * E + E], hw[0:m, c % 2, u * P:(u + 1) * P],
                                       w, start=c == 0 and u % 2 == 0, stop=c == N - 1, skip_group_check=True)
                    mm.then_inc(sm(f + "_hw_used"), 1)

                inner(0)
                hold(pe, f + "_cs", b + 1)
                for u in range(TB):
                    mm = pe.transpose(t_bf[0:48, u * P:(u + 1) * P], cs[:, u].rearrange("p c e -> p (c e)"), ident_b)
                mm.then_inc(sm(f + "_ct"), 1)
                inner(1)
                pe.wait_ge(sm(f + "_cT"), b + 1)
                for c in range(N):
                    if c < CK:
                        weights(c)
                    outer(c)
                    if c + 2 < N:
                        inner(c + 2)

        @block.tensor
        def _(pe):
            pe.wait_ge(sm("consts"), 16)
            pe.wait_ge(sm("a_w"), 64)
            pe_proj(pe, "a")
            pe_attn(pe, "a")
            pe_out(pe, "a")
            if upto >= 2:
                pe_ffn(pe, "f")
            if upto >= 3:
                pe.wait_ge(sm("b_w"), 112)
                pe_proj(pe, "b")
                pe_attn(pe, "b")
                pe_out(pe, "b")
            if upto >= 4:
                pe_ffn(pe, "h")


def constants():
    pos = np.arange(T, dtype=np.float32) + np.float32(1)
    theta = (10000.0 ** (-2.0 * np.arange(D // 2) / D)).astype(np.float32)
    ang = (pos[:, None] * theta[None, :]).astype(np.float32).reshape(TB, P, D // 2).transpose(1, 0, 2)
    cos, sin = np.cos(ang), np.sin(ang)
    i4, i16 = np.arange(4), np.arange(NE)
    c_f = np.concatenate([
        np.eye(P), np.concatenate([cos, cos], 2).reshape(P, -1), np.concatenate([sin, -sin], 2).reshape(P, -1),
        np.tile((i4[None, :] < i4[:, None]).reshape(1, -1), (P, 1)),
        np.tile((i16[None, :] < i16[:, None]).reshape(1, -1), (P, 1)), np.full((P, 1), EPS)], 1).astype(np.float32)
    r = np.arange(P)
    ms = np.where(r[None, :] > r[:, None], MASK, 0.0)
    mt = np.where(r[:, None] > r[None, :], MASK, 0.0)
    c_b = np.concatenate([np.eye(P), ms, ms, mt, mt], 1).astype(np.float32)
    e = (np.arange(ROWS) // INTER).reshape(1, CK, P)
    sel = np.tile((np.arange(NE)[:, None, None] == e), (3, 1, 1)).astype(np.float32)
    return {"c_f": c_f, "c_b": c_b, "selc": sel}


def kernel(L0_attn_a_x, L0_attn_a_Wq, L0_attn_a_bq, L0_attn_a_Wk, L0_attn_a_bk, L0_attn_a_Wv, L0_attn_a_bv,
           L0_attn_a_Wo, L0_attn_a_bo, L0_attn_b_Wq, L0_attn_b_Wk, L0_attn_b_Wv, L0_attn_b_Wo, L0_attn_b_lambda_q1,
           L0_attn_b_lambda_k1, L0_attn_b_lambda_q2, L0_attn_b_lambda_k2, L0_attn_b_subln_weight, L0_ffn_Wg,
           L0_ffn_W1, L0_ffn_W3, L0_ffn_W2, L0_ffn_Ws1, L0_ffn_Ws3, L0_ffn_Ws2, upto=4):
    import concourse.bacc as bacc
    from concourse.bass_utils import run_bass_kernel_spmd as run

    n = np.asarray
    arrays = {
        "x": n(L0_attn_a_x),
        "a_wqkv": np.concatenate([n(L0_attn_a_Wq).T, n(L0_attn_a_Wk).T, n(L0_attn_a_Wv).T], 1),
        "a_bqkv": np.concatenate([n(L0_attn_a_bq), n(L0_attn_a_bk), n(L0_attn_a_bv)]),
        "a_wo": n(L0_attn_a_Wo).T, "a_bo": n(L0_attn_a_bo),
        "b_wqkv": np.concatenate([n(L0_attn_b_Wq).T, n(L0_attn_b_Wk).T, n(L0_attn_b_Wv).T], 1),
        "b_wo": n(L0_attn_b_Wo).T, "b_g": n(L0_attn_b_subln_weight),
        "b_lq1": n(L0_attn_b_lambda_q1), "b_lk1": n(L0_attn_b_lambda_k1),
        "b_lq2": n(L0_attn_b_lambda_q2), "b_lk2": n(L0_attn_b_lambda_k2),
        "wg": n(L0_ffn_Wg).T,
        "w1": n(L0_ffn_W1).transpose(2, 0, 1).reshape(E, ROWS), "w3": n(L0_ffn_W3).transpose(2, 0, 1).reshape(E, ROWS),
        "w2": n(L0_ffn_W2).transpose(0, 2, 1).reshape(ROWS, E),
        "ws1": n(L0_ffn_Ws1).T, "ws3": n(L0_ffn_Ws3).T, "ws2": n(L0_ffn_Ws2).T,
    }
    arrays |= constants()
    arrays = {k: np.ascontiguousarray(v) for k, v in arrays.items()}
    nc = bacc.Bacc("TRN2", target_bir_lowering=False, num_devices=1)
    ins = {k: nc.dram_tensor("in_" + k, v.shape, mybir.dt.from_np(v.dtype), kind="ExternalInput").ap()
           for k, v in arrays.items()}
    out = nc.dram_tensor("out_0", (B, T, E), F32, kind="ExternalOutput").ap()
    build(nc, ins, out, upto)
    r = run(nc, [{"in_" + k: v for k, v in arrays.items()}], core_ids=[0])
    return r.results[0]["out_0"]
```

```python
from contextlib import ExitStack
import math

import numpy as np

import concourse.bass as bass
from concourse import mybir

F32 = mybir.dt.float32
BF16 = mybir.dt.bfloat16
I32 = mybir.dt.int32
ACT = mybir.ActivationFunctionType
ALU = mybir.AluOpType
X = mybir.AxisListType.X
ds = bass.ds

P = 128
B, T, E = 4, 512, 256
TB = T // P
NT = B * TB
CE = E // P
G = 8
HG = 4
D = 8
W = 64
PR = HG // 2
UNITS = 5
SBANKS = 10
RING = 8
SCALE = float(D) ** -0.5
MASK = -3.0e38
EPS = 1e-5
LAMBDA_INIT = 0.8 - 0.6 * math.exp(-0.3 * 12)
NE, INTER, SHARED = 16, 176, 352
TOPK = 4
TH = NT // 2
SLOTS = 48
assert (TH * P * TOPK + NE * (P - 1)) // P <= SLOTS and SLOTS % 4 == 0
NJ = 2 * SLOTS
SCH = [(0, 128), (128, 128), (256, 96)]
M_DMAS = 6 * 16


class Chain:

    def __init__(self, eng, sem, base=0, held=None):
        self.eng, self.sem, self.base, self.n, self.held = eng, sem, base, 0, held

    def __call__(self, ins):
        self.n += 1
        ins.then_inc(self.sem, 1)
        self.eng.wait_ge(self.sem, self.base + self.n)
        if self.held is not None:
            self.eng.sem_inc(self.held, 1)


def build(nc, ins, out):
    ctx = ExitStack()
    with ctx:
        def sb(name, shape, dt=F32):
            return ctx.enter_context(nc.sbuf_tensor(name, shape, dt))

        def sem(name):
            return ctx.enter_context(nc.semaphore(name))

        x_sb = sb("x_sb", [P, NT, E])
        y_sb = sb("y_sb", [P, NT, E])
        o_q, o_k, o_v, o_p = 0, G * NT * 32, 2 * G * NT * 32, 2 * G * NT * 32 + G * NT * 34
        o_x = CE * NE * 2 * INTER
        o_s = o_x + NT * E
        o_g = o_s + 2 * CE * SHARED + 3 * E
        o_w = o_g + 4 * E
        arena = sb("arena", [P, max(o_p + RING * 1024, o_w + 7 * 512 + 2 * INTER)])
        q_all = arena[:, o_q:o_k].rearrange("p (g t c) -> p g t c", g=G, t=NT)
        k_all = arena[:, o_k:o_v].rearrange("p (g t c) -> p g t c", g=G, t=NT)
        v_all = arena[:, o_v:o_p].rearrange("p (g t c) -> p g t c", g=G, t=NT)
        p_ring = arena[:, o_p:o_p + RING * 1024].rearrange("p (r c) -> p r c", r=RING)
        w13 = arena[:, 0:o_x].rearrange("p (c e i) -> p c e i", c=CE, e=NE)
        xnT_all = arena[:, o_x:o_s].rearrange("p (c t) -> p c t", c=CE)
        ws13 = arena[:, o_s:o_s + 2 * CE * SHARED].rearrange("p (a c r) -> p a c r", a=2, c=CE)
        ws2 = arena[:, o_g - 3 * E:o_g].rearrange("p (c e) -> p c e", c=3)
        xg = arena[:, o_g:o_w].rearrange("p (q e) -> p q e", q=4)
        xgT = arena[:, o_w:o_w + 512].rearrange("p (a c t) -> p a c t", a=2, c=CE)
        hs = arena[:, o_w + 512:o_w + 1024].rearrange("p (a i) -> p a i", a=2)
        hsT = arena[:, o_w + 1024:o_w + 1536].rearrange("p (a c t) -> p a c t", a=2, c=2)
        yt = arena[:, o_w + 1536:o_w + 2560].rearrange("p (q e) -> p q e", q=4)
        gate = arena[:, o_w + 2560:o_w + 2560 + 2 * INTER].rearrange("p (a i) -> p a i", a=2)
        r16 = arena[:, o_w:o_w + 2048].rearrange("p (a t i j) -> p a t i j", a=2, t=TB, i=NE)
        arena2 = sb("arena2", [P, 2 * 16 * T // 2])
        qT = arena2[:, 0:16 * T // 2].bitcast(BF16).rearrange("p (r t) -> p r t", r=16)
        kT = arena2[:, 16 * T // 2:].bitcast(BF16).rearrange("p (r t) -> p r t", r=16)
        w2 = arena2[:, :].rearrange("p (c e d) -> p c e d", c=2, e=NE)
        stq = sb("stq", [P, 2, 16, W], BF16)
        stk = sb("stk", [P, 2, 16, W], BF16)
        rq = sb("rq", [P, 2, 16, D])
        rk = sb("rk", [P, 2, 16, D])
        scratch = sb("scratch", [P, 3 * 320 + G * TB * 34 + T])

        def part(start, width):
            return scratch[:, start:start + width]

        raw = part(0, 320)
        tc = part(320, 320).rearrange("p (h d) -> p h d", d=D)
        tsn = part(640, 320).rearrange("p (h d) -> p h d", d=D)
        oT_sb = part(960, T)
        v_b = part(960 + T, G * TB * 34).rearrange("p (g t c) -> p g t c", g=G, t=TB)
        bm3 = sb("bm3", [P, 16, 4])
        bm2 = sb("bm2", [P, 16, 4])
        bm1 = sb("bm1", [P, 16, 2])
        nm = sb("nm", [P, TB, 16])
        nr = sb("nr", [P, 2, TB, 16])
        ms = sb("ms", [P, TB, 3, 16], BF16)
        mT = sb("mT", [48, T], BF16)
        rec = sb("rec", [P, 2, 16])
        otmp = sb("otmp", [P, 16, 16])
        osq = sb("osq", [P, TB, 32])
        ss = sb("ss", [P, NT, 16])
        lam = sb("lam", [P, 8])
        lamv = sb("lamv", [P, 4, D])
        coef = sb("coef", [P, 16])
        mv = sb("mv", [P, NT, 2])
        bst = sb("bst", [P, 2, 6])
        rstd = sb("rstd", [P, NT])
        nw = sb("nw", [P, 4, NT])
        xn = sb("xn", [P, 2, E])
        xnT = sb("xnT", [P, CE, T])
        c_f = sb("c_f", [P, 128 + 2 * TB * D + 16 + 256 + TH + SLOTS + TOPK])
        c_b = sb("c_b", [P, 128 + 256 + 256 + 256], BF16)
        wqkv = sb("wqkv", [P, CE, 768])
        wo = sb("wo", [P, CE, E])
        bqkv = sb("bqkv", [P, 384])
        bo = sb("bo", [P, E])
        gsub = sb("gsub", [P, 16])
        wg = sb("wg", [P, CE, NE])
        y_flat = y_sb[:, :, :].rearrange("p t e -> p (t e)")
        gathered = [arena[:, o_x:o_s].rearrange("p (n e) -> p n e", e=E), y_sb]
        sil = sb("sil", [P, 2, T])
        hw = sb("hw", [P, 2, T])
        sc = part(0, 2 * TH * NE).rearrange("p (a t e) -> p a t e", a=2, t=TH)
        sx = part(256, TH * NE).rearrange("p (t e) -> p t e", t=TH)
        rank = part(384, TH * NE).rearrange("p (t e) -> p t e", t=TH)
        slot = part(512, TH * NE).rearrange("p (t e) -> p t e", t=TH)
        before = part(640, (TH + 1) * NE).rearrange("p (t e) -> p t e", t=TH + 1)
        s1 = part(784, 3 * TH).rearrange("p (a t) -> p a t", a=3)
        gm = part(808, TH * 4).rearrange("p (t g) -> p t g", t=TH)
        g4 = part(840, 2 * TH * 16).rearrange("p (a t i j) -> p a t i j", a=2, t=TH, i=4)
        g1 = part(1096, 3 * TH * 4).rearrange("p (a t g) -> p a t g", a=3, t=TH)
        nt = part(1192, 4 * NE).rearrange("p (a e) -> p a e", a=4)
        slot_f = part(1256, TH * TOPK).rearrange("p (t k) -> p t k", t=TH)
        tile_f = part(1288, SLOTS)
        pick = part(1336, 2 * TH * TOPK * NE).rearrange("p (a t k e) -> p a t k e", a=2, t=TH, k=TOPK)
        taken = sb("taken", [P, TH, NE], BF16)
        slot_i = sb("slot_i", [P, NT, TOPK], I32)
        wk = sb("wk", [P, NT, TOPK])
        tile_e = sb("tile_e", [P, NJ], I32)
        zero = hw[:, 0, 0:E]
        x_slots = [nc.dram_tensor(f"x_slots{h}", (SLOTS * P, E), F32).ap() for h in range(2)]
        y_slots = [nc.dram_tensor(f"y_slots{h}", (SLOTS * P, E), F32).ap() for h in range(2)]

        st_ps = ctx.enter_context(nc.psum_tensor("st_ps", [P, 2, 1024], F32))
        s_ps = ctx.enter_context(nc.psum_tensor("s_ps", [P, 2, 512], F32))
        o_ps = ctx.enter_context(nc.psum_tensor("o_ps", [P, 512], F32))
        t_ps = ctx.enter_context(nc.psum_tensor("t_ps", [P, 512], F32))
        t_bf = t_ps[:, :].bitcast(BF16)

        ident_f = c_f[:, 0:128]
        cosT = c_f[:, 128:128 + TB * D].rearrange("p (t d) -> p t d", t=TB)
        sinT = c_f[:, 128 + TB * D:128 + 2 * TB * D].rearrange("p (t d) -> p t d", t=TB)
        o = 128 + 2 * TB * D
        low4 = c_f[:, o:o + 16]
        low16 = c_f[:, o + 16:o + 272]
        steps = c_f[:, o + 272:o + 272 + TH]
        tiles_i = c_f[:, o + 272 + TH:o + 272 + TH + SLOTS]
        ranks_i = c_f[:, o + 272 + TH + SLOTS:o + 272 + TH + SLOTS + TOPK]
        ident_b = c_b[:, 0:128]
        mask_s = c_b[:, 128:384]
        mask_t = c_b[:, 384:640]
        upper = c_b[:, 640:768]
        ones = c_b[:, 768:896]

        def out_ps(t):
            return st_ps[:, t % 2, t // 2 % 2 * 512:t // 2 % 2 * 512 + E]

        def logits_ps(hf):
            return s_ps[:, hf, 256 * hf:256 * hf + TH * NE]

        S = {}

        def sm(name):
            if name not in S:
                S[name] = sem(name)
            return S[name]

        def hold(eng, name, value):
            eng.wait_ge(sm(name), value)
            eng.sem_inc(sm("passed"), 1)

        def past(f, n):
            return n if f == "h" else 0

        block = ctx.enter_context(nc.Block())
        x_d = ins["x"].rearrange("b (t p) e -> p (b t) e", p=P)
        out_d = out.rearrange("b (t p) e -> p (b t) e", p=P)

        def sp_attn_weights(sp, s):
            n = s + "_w"
            if s == "a":
                sp.dma_start(wqkv[:, :, 0:384], ins["a_wqkv"].rearrange("(c p) n -> p c n", p=P)).then_inc(sm(n), 16)
                sp.dma_start(wo[:], ins["a_wo"].rearrange("(c p) n -> p c n", p=P)).then_inc(sm(n), 16)
                sp.dma_start(bqkv[:], ins["a_bqkv"].partition_broadcast(P)).then_inc(sm(n), 16)
                sp.dma_start(bo[:], ins["a_bo"].partition_broadcast(P)).then_inc(sm(n), 16)
            else:
                sp.dma_start(wqkv[:], ins["b_wqkv"].rearrange("(c p) n -> p c n", p=P)).then_inc(sm(n), 16)
                sp.dma_start(gsub[:], ins["b_g"].partition_broadcast(P)).then_inc(sm(n), 16)
                for j, l in enumerate(("lq1", "lk1", "lq2", "lk2")):
                    sp.dma_start(lamv[:, j, :], ins["b_" + l].partition_broadcast(P)).then_inc(sm(n), 16)

        def sp_move_maxima(sp, s):
            with sp.Fori(0, B) as b:
                for half in range(2):
                    hp = 2 * b + half
                    sp.wait_ge(sm(s + "_m_evac"), hp + 1)
                    for c in range(3):
                        for par in range(2):
                            r = 64 * par + 48 + c
                            sp.dma_start(qT[r:r + 1, 8 * half:8 * half + 8, :],
                                         mT[c * 16 + par * 8:c * 16 + par * 8 + 8, :])\
                              .then_inc(sm(s + "_m_rows"), 16)

        def sp_ffn_weights(sp, f, attn):
            sp.wait_ge(sm(attn + "_norm_done"), 1 + B * G)
            n = f + "_w"
            sp.dma_start(ws13[:, 0], ins["ws1"].rearrange("(c p) n -> p c n", p=P)).then_inc(sm(n), 16)
            sp.dma_start(ws13[:, 1], ins["ws3"].rearrange("(c p) n -> p c n", p=P)).then_inc(sm(n), 16)
            sp.dma_start(ws2[:, 0:2], ins["ws2"][0:256, :].rearrange("(c p) n -> p c n", p=P)).then_inc(sm(n), 16)
            sp.dma_start(ws2[0:96, 2], ins["ws2"][256:352, :]).then_inc(sm(n), 16)
            for c in range(CE):
                sp.dma_start(w13[:, c], ins["w13"][c * P:(c + 1) * P]).then_inc(sm(n + "e"), 16)
                sp.dma_start(w2[:, c], ins["w2"][:, c * P:(c + 1) * P, :].rearrange("e p d -> p e d"))\
                    .then_inc(sm(n + "e"), 16)

        def sp_ffn_slots(sp, f):
            def load(hf, k, q):
                sp.dma_start(xg[:, q, :], x_slots[hf][ds(k * P, P), :]).then_inc(sm(f"load{q}"), 16)

            def step(hf, k, q, load_hf, load_k):
                j = k + hf * SLOTS
                if load_hf is not None:
                    sp.wait_ge(sm("e_x_tr"), j + 1 + past(f, NJ))
                    load(load_hf, load_k, q)
                sp.wait_ge(sm("e_y_ev"), j + 1 + past(f, NJ))
                sp.dma_start(y_slots[hf][ds(k * P, P), :], yt[:, q, :]).then_inc(sm(f"store{q}"), 16)

            if f == "f":
                for q in range(4):
                    sp.sem_inc(sm(f"store{q}"), 16)
            sp.wait_ge(sm("scat0"), 16 * TH * TOPK + past(f, 16 * TH * TOPK))
            for q in range(4):
                load(0, q, q)
            for hf in range(2):
                with sp.Fori(0, SLOTS // 4 - 1) as i:
                    for q in range(4):
                        step(hf, 4 * i + q, q, hf, 4 * i + q + 4)
                if hf == 0:
                    sp.wait_ge(sm("scat1"), 16 * TH * TOPK + past(f, 16 * TH * TOPK))
                for q in range(4):
                    step(hf, SLOTS - 4 + q, q, 1 if hf == 0 else None, q)

        @block.sync
        def _(sp):
            for i in range(B):
                sp.dma_start(x_sb[:, 4 * i:4 * i + 4, :], x_d[:, 4 * i:4 * i + 4, :]).then_inc(sm(f"x_in{i}"), 16)
            sp.dma_start(c_f[:], ins["c_f"]).then_inc(sm("consts"), 16)
            sp.dma_start(y_flat[:, 0:896], ins["c_b"]).then_inc(sm("to_cast"), 16)
            sp_attn_weights(sp, "a")
            sp.dma_start(wg[:], ins["wg"].rearrange("(c p) n -> p c n", p=P)).then_inc(sm("g_w"), 16)
            sp.wait_ge(sm("zeroed"), 1)
            for h in range(2):
                with sp.Fori(0, SLOTS // 4) as i:
                    sp.dma_start(x_slots[h][ds(i * 4 * P, 4 * P), :].rearrange("(a p) e -> p a e", p=P),
                                 zero.unsqueeze(1).to_broadcast([P, 4, E])).then_inc(sm("slots_clear"), 16)
            sp_move_maxima(sp, "a")
            sp_ffn_weights(sp, "f", "a")
            sp_ffn_slots(sp, "f")
            sp.wait_ge(sm("a_out_x"), NT)
            sp_attn_weights(sp, "b")
            sp.dma_start(wo[:], ins["b_wo"].rearrange("(c p) n -> p c n", p=P)).then_inc(sm("b_w"), 16)
            sp_move_maxima(sp, "b")
            sp_ffn_weights(sp, "h", "b")
            sp_ffn_slots(sp, "h")
            with sp.Fori(0, B) as b:
                sp.wait_ge(sm("h_x"), (b + 1) * TB)
                sp.dma_start(out_d[:, ds(b * TB, TB), :], x_sb[:, ds(b * TB, TB), :]).then_inc(sm("stored"), 16)
            sp.wait_ge(sm("stored"), 16 * B)

        def pool_split(pool, s, t, g, b, wait_stack, wait_v):
            ch = Chain(pool, sm(s + "_split_chain"), t * (5 if s == "b" else 6), sm("passed"))
            par = g % 2
            q = q_all[:, g, ds(b * TB, TB), :].rearrange("p t (h d) -> p (t h) d", d=D)
            if wait_stack:
                hold(pool, s + "_tr_done", 2 * t - 3)
            st = stq[:, par]
            ch(pool.tensor_copy(st[:, :, 0:24].rearrange("p n (a d) -> p n a d", a=3),
                                q.unsqueeze(2).to_broadcast([P, 16, 3, D])))
            ch(pool.tensor_tensor(rq[:, 0], q, st[:, :, 0:8], ALU.subtract))
            pool.tensor_copy(st[:, :, 24:40].rearrange("p n (a d) -> p n a d", a=2),
                             rq[:, 0].unsqueeze(2).to_broadcast([P, 16, 2, D])).then_inc(sm(s + "_splq"), 1)
            hold(pool, s + "_splq", t + 1)
            ch(pool.tensor_tensor(rq[:, 1], rq[:, 0], st[:, :, 24:32], ALU.subtract))
            pool.tensor_copy(st[:, :, 40:48], rq[:, 1]).then_inc(sm(s + "_split_done"), 1)
            n = 16 if s == "b" else TB
            if s == "b":
                k = k_all[:, g, ds(b * TB, TB), :].rearrange("p t (h d) -> p (t h) d", d=D)
                st = stk[:, par]
            else:
                k = k_all[:, g, ds(b * TB, TB), 0:D]
                st = stk[:, par].rearrange("p (t u) w -> p t u w", u=4)[:, :, 0, :]
            if wait_stack:
                hold(pool, s + "_tr_done", 2 * t - 2)
            kr = rk[:, :, 0:n, :]
            two = st[:, :, 0:48].rearrange("p n (a c) -> p n a c", a=2)
            pool.tensor_copy(two[:, :, :, 0:8], k.unsqueeze(2).to_broadcast([P, n, 2, D])).then_inc(sm(s + "_splk"), 1)
            hold(pool, s + "_splk", 2 * t + 1)
            ch(pool.tensor_tensor(kr[:, 0], k, st[:, :, 0:8], ALU.subtract))
            pool.tensor_copy(st[:, :, 40:48], k)
            pool.tensor_copy(two[:, :, :, 8:16], kr[:, 0].unsqueeze(2).to_broadcast([P, n, 2, D]))\
                .then_inc(sm(s + "_splk"), 1)
            hold(pool, s + "_splk", 2 * t + 2)
            ch(pool.tensor_tensor(kr[:, 1], kr[:, 0], st[:, :, 8:16], ALU.subtract))
            last = pool.tensor_copy(st[:, :, 16:24], kr[:, 1])
            if s == "a":
                ch(last)
                last = pool.tensor_copy(stk[:, par].rearrange("p (t u) w -> p t u w", u=4)[:, :, 1, 0:48],
                                        st[:, :, 0:48])
            last.then_inc(sm(s + "_split_done"), 1)
            hold(pool, s + "_split_done", 2 * t + 2)
            vw = 34 if s == "b" else 9
            if wait_v:
                hold(pool, s + "_p_free", 5 * t - 27)
            pool.tensor_copy(v_b[:, g, :, 0:vw], v_all[:, g, ds(b * TB, TB), 0:vw]).then_inc(sm(s + "_v_done"), 1)

        def pool_attn(pool, s):
            if s == "a":
                pool.wait_ge(sm("a_proj_done"), NT)
            else:
                pool.wait_ge(sm("b_ps_free"), 2 + NT)
            for g in range(G):
                pool_split(pool, s, g, g, 0, g >= 2, False)
            with pool.Fori(0, B - 1) as b:
                for g in range(G):
                    pool_split(pool, s, 8 * b + g + 8, g, b + 1, True, True)

        def pool_ffn(pool, f):
            for hf in range(2):
                pool.wait_ge(sm("e_slots"), hf + 1 + past(f, 2))
                if hf == 0:
                    pool.wait_ge(sm("slots_clear"), 16 * (NJ // 4))
                for t in range(hf * TH, hf * TH + TH):
                    for k in range(TOPK):
                        pool.indirect_dma_start(x_slots[hf], bass.IndirectOffsetOnAxis(ap=slot_i[:, t, k:k + 1], axis=0),
                                                y_sb[:, t, :], None).then_inc(sm(f"scat{hf}"), 16)
            for hf in range(2):
                for q in range(4):
                    pool.wait_ge(sm(f"store{q}"), 16 * (1 + (hf + 1) * SLOTS // 4) + past(f, 16 * NJ // 4))
                if hf == 0:
                    pool.wait_ge(sm("scat1"), 16 * TH * TOPK + past(f, 16 * TH * TOPK))
                for t in range(hf * TH, hf * TH + TH):
                    if hf == 1:
                        pool.wait_ge(sm(f + "_x"), t - TH + 1)
                    for k in range(TOPK):
                        n = (t % TH) * TOPK + k
                        pool.indirect_dma_start(gathered[n // 16][:, n % 16, :], None, y_slots[hf],
                                                bass.IndirectOffsetOnAxis(ap=slot_i[:, t, k:k + 1], axis=0))\
                            .then_inc(sm(f"back{t % TH}"), 16)

        @block.gpsimd
        def _(pool):
            pool.memset(zero, 0.0).then_inc(sm("zeroed"), 1)
            pool.memset(stq[:, :, :, 48:64], 0.0).then_inc(sm("st_init"), 1)
            pool.memset(stk[:, :, :, 51:64], 0.0).then_inc(sm("st_init"), 1)
            pool.memset(stk[:, :, :, 48:51], 1.0).then_inc(sm("st_init"), 1)
            pool.memset(v_all[:, :, :, D:D + 1], 1.0).then_inc(sm("a_ones"), 1)
            pool.wait_ge(sm("st_init"), 3)
            pool.wait_ge(sm("a_ones"), 1)
            pool_attn(pool, "a")
            pool_ffn(pool, "f")
            pool.wait_ge(sm("f_x"), NT)
            vo = v_all.rearrange("p g t (h c) -> p g t h c", h=2)
            pool.memset(vo[:, :, :, :, 16:17], 1.0).then_inc(sm("b_ones"), 1)
            pool.wait_ge(sm("b_ones"), 1)
            pool_attn(pool, "b")
            pool_ffn(pool, "h")

        def act_sqrt(act, s):
            act.wait_ge(sm(s + "_var"), 1)
            act.activation(nw[:, 0, :], nw[:, 1, :], ACT.Sqrt).then_inc(sm(s + "_std"), 1)

        def act_tile_T(act, s, t, u):
            src = t_ps if u % 2 == 0 else o_ps
            act.wait_ge(sm(s + "_xt"), t + 1)
            act.activation(xnT[:, :, u * P:(u + 1) * P], src[:, 0:256].rearrange("p (c t) -> p c t", c=CE),
                           ACT.Copy).then_inc(sm(s + "_xnT"), 1)

        def act_proj(act, s):
            act_sqrt(act, s)
            with act.Fori(0, B) as b:
                for u in range(TB):
                    t = TB * b + u
                    act_tile_T(act, s, t, u)
                    if s == "b":
                        act.wait_ge(sm("b_qkv"), 2 * t + 1)
                        act.activation(q_all[:, :, ds(t, 1), :].rearrange("p g t c -> p (g t) c"),
                                       st_ps[:, u % 2, 0:256].rearrange("p (g c) -> p g c", g=G),
                                       ACT.Copy).then_inc(sm("b_q_copied"), 1)

        def act_slot(act, s, n, g, t):
            for u in range(UNITS):
                U = 5 * n + u
                act.wait_ge(sm(s + "_st_done"), U + 1)
                act.wait_ge(sm(s + "_p_free"), U + 1)
                r = (5 * g + u) % RING
                act.activation(p_ring[:, r, :], st_ps[:, (5 * g + u) % 2, :], ACT.Exp, scale=SCALE)\
                    .then_inc(sm(s + "_exp_done"), 1)
            if t is not None:
                act_q_evac(act, s, t, g)
            act.wait_ge(sm(s + "_p_free"), RING + 5 * n + 5)
            act.activation(oT_sb[:], o_ps[:], ACT.Copy).then_inc(sm(s + "_ot_evac"), 1)

        def act_q_evac(act, s, t, g):
            act.wait_ge(sm(s + "_tr_done"), 2 * t + 1)
            act.activation(qT[:, 2 * g:2 * g + 2, :], t_bf.rearrange("p (r t) -> p r t", r=2), ACT.Copy)\
                .then_inc(sm(s + "_q_evac"), 1)

        def act_attn(act, s):
            act.sem_inc(sm(s + "_exp_done"), 2)
            if s == "b":
                act.wait_ge(sm("b_lam"), 1)
                act.activation(lam[:, 2:4], lam[:, 0:2], ACT.Exp).then_inc(sm("b_lam_exp"), 1)
            for g in range(G):
                act_q_evac(act, s, g, g)
            with act.Fori(0, B - 1) as b:
                for g in range(G):
                    act_slot(act, s, 8 * b + g, g, 8 * b + g + 8)
            for g in range(G):
                act_slot(act, s, 8 * (B - 1) + g, g, None)

        def act_out(act, s):
            if s == "b":
                act.wait_ge(sm("b_ms"), 1)
                act.activation(ss[:], ss[:], ACT.Sqrt).then_inc(sm("b_ms_std"), 1)
            for t in range(NT):
                act.wait_ge(sm(s + "_yt"), t + 1)
                if t >= 4:
                    act.wait_ge(sm(s + "_po"), t - 3)
                act.activation(xnT[:, :, t % 4 * P:t % 4 * P + P],
                               (t_ps if t % 2 == 0 else o_ps)[:, 0:256].rearrange("p (c t) -> p c t", c=CE),
                               ACT.Copy).then_inc(sm(s + "_yT"), 1)

        def act_ffn(act, f):
            act_sqrt(act, f)
            for t in range(NT):
                src = t_ps if t % 2 == 0 else o_ps
                act.wait_ge(sm("e_xt"), t + 1 + past(f, NT))
                act.activation(xnT_all[:, :, t * P:(t + 1) * P], src[:, 0:256].rearrange("p (c t) -> p c t", c=CE),
                               ACT.Copy).then_inc(sm("e_xnT"), 1)
            for k in range(3 * B):
                if k == 0 or k == 2:
                    act.wait_ge(sm("e_sx"), k // 2 + 1 + past(f, 2))
                    act.activation(sc[:, k // 2], sx[:], ACT.Exp).then_inc(sm("e_sexp"), 1)
                act.wait_ge(sm("e_h"), k + 1 + past(f, 3 * B))
                act.wait_ge(sm(f + "_sil_free"), k + 1)
                m = SCH[k % 3][1]
                act.activation(sil[0:m, k % 2, :], st_ps[0:m, k % 2, 0:512], ACT.Silu).then_inc(sm("e_sil"), 1)

            def tile_in(j, q):
                act.wait_ge(sm("e_x_tr"), j + 1 + past(f, NJ))
                act.activation(xgT[:, q % 2], (t_ps if q % 2 == 0 else o_ps)[:, 0:256].rearrange("p (c t) -> p c t", c=CE),
                               ACT.Copy).then_inc(sm("e_x_ev"), 1)

            def silu(j, q):
                act.wait_ge(sm("e_h1"), j + 1 + past(f, NJ))
                act.activation(gate[:, q % 2, :], s_ps[:, q % 2, 0:INTER], ACT.Silu).then_inc(sm("e_gate"), 1)

            tile_in(0, 0)
            tile_in(1, 1)
            silu(0, 0)
            with act.Fori(0, NJ // 4 - 1) as i:
                for q in range(4):
                    tile_in(4 * i + q + 2, q + 2)
                    silu(4 * i + q + 1, q + 1)
            for q in range(4):
                if q < 2:
                    tile_in(NJ - 4 + q + 2, q + 2)
                if q < 3:
                    silu(NJ - 4 + q + 1, q + 1)

        @block.scalar
        def _(act):
            act_proj(act, "a")
            act_attn(act, "a")
            act_out(act, "a")
            act_ffn(act, "f")
            act_proj(act, "b")
            act_attn(act, "b")
            act_out(act, "b")
            act_ffn(act, "h")

        straight = {}

        def straight_chain(dve):
            if "dve" not in straight:
                straight["dve"] = Chain(dve, sm("straight"))
            return straight["dve"]

        def dve_stats(dve, section, t):
            n = NT * section + t
            ch = Chain(dve, sm("st_chain"), 2 * n, sm("passed"))
            xt = x_sb[:, ds(t, 1), :].rearrange("p a e -> p (a e)")
            ch(dve.bn_stats(bst[:, 0, :], xt))
            ch(dve.bn_aggr(bst[:, 1, 0:2], bst[:, 0, :]))
            dve.tensor_copy(mv[:, ds(t, 1), :].rearrange("p a e -> p (a e)"), bst[:, 1, 0:2])\
                .then_inc(sm("stats"), 1)
            dve.wait_ge(sm("stats"), n + 1)

        def dve_rstd(dve, s):
            ch = straight_chain(dve)
            dve.tensor_scalar(nw[:, 1, :], mv[:, :, 1], EPS, None, ALU.add).then_inc(sm(s + "_var"), 1)
            dve.wait_ge(sm(s + "_std"), 1)
            ch(dve.reciprocal(nw[:, 2, :], nw[:, 0, :]))
            ch(dve.tensor_tensor(nw[:, 3, :], nw[:, 2, :], nw[:, 2, :], ALU.mult))
            ch(dve.tensor_tensor(nw[:, 3, :], nw[:, 3, :], nw[:, 1, :], ALU.mult))
            ch(dve.tensor_scalar(nw[:, 3, :], nw[:, 3, :], -0.5, 1.5, ALU.mult, ALU.add))
            ch(dve.tensor_tensor(rstd[:], nw[:, 2, :], nw[:, 3, :], ALU.mult))

        def dve_ln(dve, s, t, u):
            dve.tensor_scalar(xn[:, u % 2, :], x_sb[:, ds(t, 1), :].rearrange("p a e -> p (a e)"),
                              mv[:, ds(t, 1), 0:1].rearrange("p a e -> p (a e)"), rstd[:, ds(t, 1)],
                              ALU.subtract, ALU.mult).then_inc(sm(s + "_xn"), 1)

        def dve_proj_tile(dve, s, t, u, ahead):
            ps = st_ps[:, u % 2, :]
            tile = ds(t, 1)
            if ahead:
                hold(dve, s + "_xt", t + 1)
                dve_ln(dve, s, t + 2, u)
            if s == "a":
                ch = Chain(dve, sm("a_rope"), t * 3)
                dve.wait_ge(sm("a_qkv"), t + 1)
                ch(dve.tensor_tensor(raw[:], ps[:, 0:320], bqkv[:, 0:320], ALU.add))
                dve.tensor_tensor(v_all[:, :, tile, 0:D].rearrange("p g t c -> p (g t) c"),
                                  ps[:, 320:384].rearrange("p (g c) -> p g c", g=G),
                                  bqkv[:, 320:384].rearrange("p (g c) -> p g c", g=G), ALU.add)\
                    .then_inc(sm("a_ps_free"), 1)
                r3 = raw[:].rearrange("p (h d) -> p h d", d=D)
                ch(dve.tensor_tensor(tc[:], r3, cosT[:, u:u + 1, :].to_broadcast([P, 40, D]), ALU.mult))
                ch(dve.tensor_tensor(tsn[:], r3, sinT[:, u:u + 1, :].to_broadcast([P, 40, D]), ALU.mult))
                for lo in range(2):
                    a, c = 4 * lo, 4 - 4 * lo
                    qo = q_all[:, :, tile, :].rearrange("p g t (h d) -> p (g t) h d", d=D)
                    dve.tensor_tensor(qo[:, :, :, a:a + 4],
                                      tc[:, 0:32, a:a + 4].rearrange("p (g h) d -> p g h d", g=G),
                                      tsn[:, 0:32, c:c + 4].rearrange("p (g h) d -> p g h d", g=G), ALU.add)
                    last = dve.tensor_tensor(k_all[:, :, tile, a:a + 4].rearrange("p g t c -> p (g t) c"),
                                             tc[:, 32:40, a:a + 4], tsn[:, 32:40, c:c + 4], ALU.add)
                last.then_inc(sm("a_proj_done"), 1)
                dve.wait_ge(sm("a_proj_done"), t + 1)
            else:
                dve.wait_ge(sm("b_qkv"), 2 * t + 1)
                dve.wait_ge(sm("b_q_copied"), t + 1)
                dve.tensor_copy(k_all[:, :, tile, :].rearrange("p g t c -> p (g t) c"),
                                ps[:, 256:512].rearrange("p (g c) -> p g c", g=G))
                dve.wait_ge(sm("b_qkv"), 2 * t + 2)
                for h in range(2):
                    last = dve.tensor_copy(v_all[:, :, tile, 17 * h:17 * h + 16].rearrange("p g t c -> p (g t) c"),
                                           ps[:, 512:768].rearrange("p (g h c) -> p g h c", g=G, h=2)[:, :, h, :])
                last.then_inc(sm("b_ps_free"), 1)

        def dve_proj(dve, s):
            dve_rstd(dve, s)
            dve.wait_ge(sm("consts"), 16)
            dve.wait_ge(sm(s + "_w"), 64 if s == "a" else 112)
            dve_ln(dve, s, 0, 0)
            dve_ln(dve, s, 1, 1)
            with dve.Fori(0, B - 1) as b:
                for u in range(TB):
                    dve_proj_tile(dve, s, TB * b + u, u, True)
            for u in range(TB):
                dve_proj_tile(dve, s, TB * (B - 1) + u, u, u < 2)

        def dve_max(dve, s, n, g, k):
            h0 = HG * (g % 4)
            if k < 4:
                dst = bm3[:, h0 + k, :]
            elif k < 8:
                dst = bm2[:, h0 + k - 4, :]
            else:
                dst = bm1[:, h0:h0 + 4, :].rearrange("p (j a) c -> p a j c", a=2)[:, k - 8]
            dve.wait_ge(sm(s + "_s_done"), 10 * n + k + 1)
            src = s_ps[:, k % 2, :]
            src = src.rearrange("p (c k) -> p c k", c=4) if k < 8 else src.rearrange("p (j c k) -> p j c k", j=2, c=2)
            dve.tensor_reduce(dst, src, X, ALU.max)\
                .then_inc(sm(s + "_max_done"), 1)

        def dve_maxima(dve, s, hp):
            ch = Chain(dve, sm(s + "_m_chain"), hp * 8)

            def to(i):
                return nm[:, i, :].rearrange("p (par pr) -> p pr par", par=2)

            dve.wait_ge(sm(s + "_max_done"), (4 * hp + 4) * 10 + 2)
            ch(dve.tensor_reduce(to(3), bm3[:].rearrange("p (pr par) k -> p pr par k", par=2), X, ALU.max, negate=True))
            ch(dve.tensor_reduce(to(2), bm2[:, :, 0:3].rearrange("p (pr par) k -> p pr par k", par=2), X, ALU.max,
                                 negate=True))
            ch(dve.tensor_reduce(to(1), bm1[:].rearrange("p (pr par) k -> p pr par k", par=2), X, ALU.max, negate=True))
            ch(dve.tensor_scalar(to(0), bm2[:, :, 3].rearrange("p (pr par) -> p pr par", par=2), -1.0, None, ALU.mult))
            ch(dve.tensor_copy(ms[:, :, 0, :], nm[:]))
            ch(dve.tensor_tensor(nr[:, 0], nm[:], ms[:, :, 0, :], ALU.subtract))
            ch(dve.tensor_copy(ms[:, :, 1, :], nr[:, 0]))
            ch(dve.tensor_tensor(nr[:, 1], nr[:, 0], ms[:, :, 1, :], ALU.subtract))
            dve.tensor_copy(ms[:, :, 2, :], nr[:, 1]).then_inc(sm(s + "_m_split"), 1)

        def dve_m_evac(dve, s, hp, first=False):
            dve.wait_ge(sm(s + "_m_tr"), hp + 1)
            if not first:
                dve.wait_ge(sm(s + "_m_rows"), M_DMAS * hp)
            dve.tensor_copy(mT[:], t_bf[0:48, 0:T]).then_inc(sm(s + "_m_evac"), 1)

        def dve_k_evac(dve, s, t, g):
            dve.wait_ge(sm(s + "_tr_done"), 2 * t + 2)
            if s == "b":
                dve.tensor_copy(kT[:, 2 * g:2 * g + 2, :], t_bf.rearrange("p (r t) -> p r t", r=2))\
                    .then_inc(sm(s + "_k_evac"), 1)
            else:
                dve.tensor_copy(kT[:, g, :], t_bf[:, 0:T]).then_inc(sm(s + "_k_evac"), 1)

        def dve_norm(dve, s, n, g, b):
            o3 = t_ps[:, :].rearrange("p (n c) -> p n c", c=32)
            dve.wait_ge(sm(s + "_otr_done"), n + 1)
            tiles = ds(b * TB, TB)
            if s == "a":
                ch = Chain(dve, sm("a_norm_chain"), n)
                ch(dve.reciprocal(rec[:, 0, :], o3[:, :, D]))
                dve.tensor_tensor(y_sb[:, tiles, 32 * g:32 * g + 32].rearrange("p t (h d) -> p t h d", d=D),
                                  o3[:, :, 0:D].rearrange("p (t h) d -> p t h d", t=TB),
                                  rec[:, 0, :].rearrange("p (t h) -> p t h", t=TB).unsqueeze(3).to_broadcast([P, TB, HG, D]),
                                  ALU.mult).then_inc(sm("a_norm_done"), 1)
                dve.wait_ge(sm("a_norm_done"), n + 2)
            else:
                ch = Chain(dve, sm("b_norm_chain"), n * 5)
                ch(dve.reciprocal(rec[:, 0, :], o3[:, :, 16]))
                ch(dve.tensor_tensor(rec[:, 1, :], rec[:, 0, :], coef[:], ALU.mult))
                dve.tensor_tensor(otmp[:], o3[:, :, 0:16], rec[:, 1, :].unsqueeze(2).to_broadcast([P, 16, 16]),
                                  ALU.mult).then_inc(sm("b_norm_done"), 1)
                dve.wait_ge(sm("b_norm_done"), n + 2)
                o5 = otmp[:].rearrange("p (t h a) c -> p t h a c", t=TB, a=2)
                yv = y_sb[:, tiles, 32 * g:32 * g + 32]
                ch(dve.tensor_tensor(yv.rearrange("p t (h c) -> p t h c", h=2), o5[:, :, :, 0, :], o5[:, :, :, 1, :],
                                     ALU.add))
                ch(dve.tensor_tensor(osq[:], yv, yv, ALU.mult))
                ch(dve.tensor_reduce(ss[:, tiles, 2 * g:2 * g + 2], osq[:].rearrange("p t (h c) -> p t h c", h=2),
                                     X, ALU.add))

        def dve_slot(dve, s, n, g, b, with_s, with_t):
            sn, sg = n + 7, (g - 1) % G
            if g == 1:
                dve_m_evac(dve, s, 2 * b + 1)
            if g == 5 and with_t:
                dve_m_evac(dve, s, 2 * b + 2)
            if with_s:
                for k in range(7):
                    dve_max(dve, s, sn, sg, k)
            if with_t:
                dve_k_evac(dve, s, n + 8, g)
            if with_s:
                for k in range(7, SBANKS):
                    dve_max(dve, s, sn, sg, k)
            dve_norm(dve, s, n, g, b)
            if with_s and sg == 3:
                dve_maxima(dve, s, 2 * b + 2)
            if with_s and sg == 7:
                dve_maxima(dve, s, 2 * b + 1)

        def dve_attn(dve, s):
            dve.sem_inc(sm(s + "_max_done"), 2)
            dve.sem_inc(sm(s + "_norm_done"), 1)
            dve.memset(o_ps[:], 0.0).then_inc(sm(s + "_o_init"), 1)
            if s == "b":
                ch = Chain(dve, sm("b_lam_chain"))
                ch(dve.tensor_tensor(lamv[:, 0, :], lamv[:, 0, :], lamv[:, 1, :], ALU.mult))
                ch(dve.tensor_tensor(lamv[:, 2, :], lamv[:, 2, :], lamv[:, 3, :], ALU.mult))
                dve.tensor_reduce(lam[:, 0:2], lamv[:].rearrange("p (a c) d -> p a c d", c=2)[:, :, 0, :], X, ALU.add)\
                    .then_inc(sm("b_lam"), 1)
                dve.wait_ge(sm("b_lam_exp"), 1)
                ch(dve.tensor_tensor(lam[:, 4:5], lam[:, 3:4], lam[:, 2:3], ALU.subtract))
                ch(dve.tensor_scalar(lam[:, 5:6], lam[:, 4:5], -LAMBDA_INIT, None, ALU.add))
                ch(dve.memset(coef[:], 1.0))
                cv = coef[:].rearrange("p (n a) -> p n a", a=2)
                ch(dve.tensor_scalar(cv[:, :, 1], cv[:, :, 1], lam[:, 5:6], None, ALU.mult))
            dve_k_evac(dve, s, 0, 0)
            for g in range(G - 1):
                if g == 4:
                    dve_m_evac(dve, s, 0, first=True)
                for k in range(SBANKS):
                    dve_max(dve, s, g, g, k)
                if g == 3:
                    dve_maxima(dve, s, 0)
                dve_k_evac(dve, s, g + 1, g + 1)
            with dve.Fori(0, B - 1) as b:
                for g in range(G):
                    dve_slot(dve, s, 8 * b + g, g, b, True, True)
            for g in range(G):
                dve_slot(dve, s, 8 * (B - 1) + g, g, B - 1, g == 0, False)

        def dve_out(dve, s):
            ch = straight_chain(dve)
            if s == "b":
                dve.wait_ge(sm("b_norm_chain"), 5 * B * G)
                dve.tensor_scalar(ss[:], ss[:], 1.0 / 16, EPS, ALU.mult, ALU.add).then_inc(sm("b_ms"), 1)
                dve.wait_ge(sm("b_ms_std"), 1)
                ch(dve.reciprocal(ss[:], ss[:]))
                ch(dve.tensor_scalar(gsub[:], gsub[:], 1.0 - LAMBDA_INIT, None, ALU.mult))

            def prepare(t):
                if s == "a":
                    ch(dve.tensor_tensor(x_sb[:, t, :], x_sb[:, t, :], bo[:], ALU.add))
                else:
                    y = y_sb[:, t, :].rearrange("p (h c) -> p h c", h=16)
                    ch(dve.tensor_tensor(y, y, ss[:, t, :].unsqueeze(2).to_broadcast([P, 16, 16]), ALU.mult))
                    dve.tensor_tensor(y, y, gsub[:].unsqueeze(1).to_broadcast([P, 16, 16]), ALU.mult)\
                        .then_inc(sm("b_y"), 1)

            for t in range(3):
                prepare(t)
            for t in range(NT):
                if t + 3 < NT:
                    prepare(t + 3)
                dve.wait_ge(sm(s + "_po"), t + 1)
                dve.tensor_tensor(x_sb[:, t, :], x_sb[:, t, :], out_ps(t), ALU.add).then_inc(sm(s + "_out_x"), 1)
                dve.wait_ge(sm(s + "_out_x"), t + 1)
                dve_stats(dve, 1 if s == "a" else 3, t)

        def dve_ffn(dve, f):
            ch = straight_chain(dve)
            dve_rstd(dve, f)
            for t in range(NT):
                dve.tensor_scalar(y_sb[:, t, :], x_sb[:, t, :], mv[:, t, 0:1], rstd[:, t:t + 1],
                                  ALU.subtract, ALU.mult).then_inc(sm("e_xn"), 1)

            def scores(hf):
                lg = logits_ps(hf).rearrange("p (t e) -> p t e", t=TH)
                w = sc[:, hf]
                dve.wait_ge(sm("e_lg"), hf + 1 + past(f, 2))
                ch(dve.tensor_reduce(s1[:, 0, :], lg, X, ALU.max))
                dve.tensor_tensor(sx[:], lg, s1[:, 0, :].unsqueeze(2).to_broadcast([P, TH, NE]), ALU.subtract)\
                    .then_inc(sm("e_sx"), 1)
                dve.wait_ge(sm("e_sexp"), hf + 1 + past(f, 2))
                ch(dve.tensor_reduce(s1[:, 1, :], w, X, ALU.add))
                ch(dve.reciprocal(s1[:, 2, :], s1[:, 1, :]))
                ch(dve.tensor_tensor(w, w, s1[:, 2, :].unsqueeze(2).to_broadcast([P, TH, NE]), ALU.mult))
                ch(dve.tensor_reduce(gm[:], w.rearrange("p t (g e) -> p t g e", g=4), X, ALU.max))
                gj = gm[:].unsqueeze(2).to_broadcast([P, TH, 4, 4])
                gi = gm[:].unsqueeze(3).to_broadcast([P, TH, 4, 4])
                l4 = low4.unsqueeze(1).to_broadcast([P, TH, 16])
                f4 = g4[:, 1].rearrange("p t i j -> p t (i j)")
                ch(dve.tensor_tensor(g4[:, 0], gj, gi, ALU.is_gt))
                ch(dve.tensor_tensor(g4[:, 1], gj, gi, ALU.is_equal))
                ch(dve.tensor_tensor(f4, f4, l4, ALU.mult))
                ch(dve.tensor_tensor(g4[:, 0], g4[:, 0], g4[:, 1], ALU.add))
                ch(dve.tensor_reduce(g1[:, 0], g4[:, 0], X, ALU.add))
                ch(dve.tensor_scalar(g1[:, 1], g1[:, 0], 2.0, None, ALU.is_lt))
                ch(dve.tensor_scalar(g1[:, 2], g1[:, 1], -1.0, None, ALU.add))
                sv = sx[:].rearrange("p t (g e) -> p t g e", g=4)
                ch(dve.tensor_tensor(sv, w.rearrange("p t (g e) -> p t g e", g=4),
                                     g1[:, 1].unsqueeze(3).to_broadcast([P, TH, 4, 4]), ALU.mult))
                ch(dve.tensor_tensor(sv, sv, g1[:, 2].unsqueeze(3).to_broadcast([P, TH, 4, 4]), ALU.add))

            def ranks(h):
                part = sx[:, TB * h:TB * h + TB, :]
                sj = part.unsqueeze(2).to_broadcast([P, TB, NE, NE])
                si = part.unsqueeze(3).to_broadcast([P, TB, NE, NE])
                f1 = r16[:, 1].rearrange("p t i j -> p t (i j)")
                ch(dve.tensor_tensor(r16[:, 0], sj, si, ALU.is_gt))
                ch(dve.tensor_tensor(r16[:, 1], sj, si, ALU.is_equal))
                ch(dve.tensor_tensor(f1, f1, low16.unsqueeze(1).to_broadcast([P, TB, 256]), ALU.mult))
                ch(dve.tensor_tensor(r16[:, 0], r16[:, 0], r16[:, 1], ALU.add))
                ch(dve.tensor_reduce(rank[:, TB * h:TB * h + TB, :], r16[:, 0], X, ALU.add))
                if h == 1:
                    dve.tensor_scalar(taken[:], rank[:], float(TOPK), None, ALU.is_lt).then_inc(sm("e_taken"), 1)

            def slots(hf):
                inside = s_ps[:, 1, 0:P].rearrange("p (t e) -> p t e", t=TH)
                total = s_ps[:, 1, P:2 * P].rearrange("p (t e) -> p t e", t=TH)
                ch(dve.memset(before[:, 0, :], 0.0))
                dve.wait_ge(sm("e_counts"), hf + 1 + past(f, 2))
                for t in range(TH):
                    ch(dve.tensor_tensor(before[:, t + 1, :], before[:, t, :], total[:, t, :], ALU.add))
                flat = r16.rearrange("p a t i j -> p (a t i j)")
                c8 = flat[:, 0:NE * TH].rearrange("p (e k) -> p e k", e=NE)
                ch(dve.tensor_tensor(c8, before[:, TH, :].unsqueeze(2).to_broadcast([P, NE, TH]),
                                     steps.unsqueeze(1).to_broadcast([P, NE, TH]), ALU.is_gt))
                ch(dve.tensor_reduce(nt[:, 0, :], c8, X, ALU.add))
                c16 = flat[:, 0:NE * NE].rearrange("p (i j) -> p i j", i=NE)
                ch(dve.tensor_tensor(c16, low16.rearrange("p (i j) -> p i j", i=NE),
                                     nt[:, 0, :].unsqueeze(1).to_broadcast([P, NE, NE]), ALU.mult))
                ch(dve.tensor_reduce(nt[:, 1, :], c16, X, ALU.add))
                ch(dve.tensor_tensor(nt[:, 2, :], nt[:, 0, :], nt[:, 1, :], ALU.add))
                ch(dve.tensor_scalar(nt[:, 3, :], nt[:, 1, :], float(P), None, ALU.mult))
                ch(dve.tensor_tensor(slot[:], inside, before[:, 0:TH, :], ALU.add))
                ch(dve.tensor_tensor(slot[:], slot[:], nt[:, 3, :].unsqueeze(1).to_broadcast([P, TH, NE]), ALU.add))

            def assign(hf):
                flat = r16.rearrange("p a t i j -> p (a t i j)")
                sh = [P, TH, TOPK, NE]
                ch(dve.tensor_tensor(pick[:, 0], rank[:].unsqueeze(2).to_broadcast(sh),
                                     ranks_i.unsqueeze(1).unsqueeze(3).to_broadcast(sh), ALU.is_equal))
                ch(dve.tensor_tensor(pick[:, 1], pick[:, 0], slot[:].unsqueeze(2).to_broadcast(sh), ALU.mult))
                ch(dve.tensor_reduce(slot_f[:], pick[:, 1], X, ALU.add))
                dve.tensor_copy(slot_i[:, hf * TH:hf * TH + TH, :], slot_f[:]).then_inc(sm("e_slots"), 1)
                ch(dve.tensor_tensor(pick[:, 0], pick[:, 0], sc[:, hf].unsqueeze(2).to_broadcast(sh), ALU.mult))
                ch(dve.tensor_reduce(wk[:, hf * TH:hf * TH + TH, :], pick[:, 0], X, ALU.add))
                c48 = flat[:, 0:SLOTS * NE].rearrange("p (j e) -> p j e", e=NE)
                ch(dve.tensor_tensor(c48, tiles_i.unsqueeze(2).to_broadcast([P, SLOTS, NE]),
                                     nt[:, 2, :].unsqueeze(1).to_broadcast([P, SLOTS, NE]), ALU.is_ge))
                ch(dve.tensor_reduce(tile_f[:], c48, X, ALU.add))
                ch(dve.tensor_scalar(tile_e[:, hf * SLOTS:(hf + 1) * SLOTS], tile_f[:], float(NE - 1), None, ALU.min))

            def add_shared(b):
                dve.wait_ge(sm(f + "_hw_used"), 3 * b + 3 + 2)
                for u in range(TB):
                    t = TB * b + u
                    dve.tensor_tensor(x_sb[:, t, :], x_sb[:, t, :],
                                      (t_ps if u < 2 else o_ps)[:, (u % 2) * E:(u % 2) * E + E], ALU.add)\
                        .then_inc(sm("e_z_free"), 1)

            scores(0)
            ranks(0)
            ranks(1)
            for k in range(3 * B):
                m = SCH[k % 3][1]
                dve.wait_ge(sm("e_sil"), k + 1 + past(f, 3 * B))
                dve.wait_ge(sm(f + "_hw_used"), k + 1)
                dve.tensor_tensor(hw[0:m, k % 2, :], sil[0:m, k % 2, :], st_ps[0:m, k % 2, 512:1024], ALU.mult)\
                    .then_inc(sm(f + "_sil_free"), 1)
                if k % 3 == 0 and k > 0:
                    add_shared(k // 3 - 1)
                if k == 0:
                    slots(0)
                    assign(0)
                if k == 1:
                    scores(1)
                if k == 2 or k == 3:
                    ranks(k - 2)
                if k == 5:
                    slots(1)
                if k == 6:
                    assign(1)
            add_shared(B - 1)
            dve.wait_ge(sm("e_z_free"), NT + past(f, NT))
            dve.memset(hs[:, :, INTER:E], 0.0).then_inc(sm("e_hs0"), 1)
            dve.wait_ge(sm("e_hs0"), 1 + past(f, 1))

            def inner(j, q):
                dve.wait_ge(sm("e_gate"), j + 1 + past(f, NJ))
                dve.tensor_tensor(hs[:, q % 2, 0:INTER], gate[:, q % 2, :], s_ps[:, q % 2, INTER:2 * INTER], ALU.mult)\
                    .then_inc(sm("e_hs"), 1)

            def turned(j, q):
                dve.wait_ge(sm("e_h_tr"), j + 1 + past(f, NJ))
                dve.tensor_copy(hsT[:, q % 2], st_ps[:, q % 2, 0:256].rearrange("p (c t) -> p c t", c=2))\
                    .then_inc(sm("e_hT_ev"), 1)

            def result(j, q):
                dve.wait_ge(sm("e_y_mm"), j + 1 + past(f, NJ))
                dve.wait_ge(sm(f"store{q % 4}"), 4 * (j - q % 4) + 16 + past(f, 16 * NJ // 4))
                dve.tensor_copy(yt[:, q % 4, :], st_ps[:, q % 2, 512:512 + E]).then_inc(sm("e_y_ev"), 1)

            def add_result(t, k):
                if k == 0:
                    dve.wait_ge(sm(f"back{t % TH}"), 16 * TOPK * (1 + t // TH + past(f, 2)))
                else:
                    dve.wait_ge(sm("summed"), (TOPK - 1) * t + k + past(f, (TOPK - 1) * NT))
                n = (t % TH) * TOPK + k
                dve.scalar_tensor_tensor(x_sb[:, t, :], gathered[n // 16][:, n % 16, :], wk[:, t, k:k + 1],
                                         x_sb[:, t, :], ALU.mult, ALU.add)\
                    .then_inc(sm("summed") if k < TOPK - 1 else sm(f + "_x"), 1)

            inner(0, 0)
            with dve.Fori(0, NJ // 4 - TH) as i:
                for q in range(4):
                    j = 4 * i + q
                    turned(j, q)
                    inner(j + 1, q + 1)
                    result(j, q)
            for q in range(4 * TH):
                j = NJ - 4 * TH + q
                turned(j, q)
                if j < NJ - 1:
                    inner(j + 1, q + 1)
                result(j, q)
                add_result(q // TOPK, q % TOPK)
            for t in range(NT):
                if t >= TH:
                    for k in range(TOPK):
                        add_result(t, k)
                if f == "f":
                    dve.wait_ge(sm("f_x"), t + 1)
                    dve_stats(dve, 2, t)

        @block.vector
        def _(dve):
            dve.wait_ge(sm("to_cast"), 16)
            dve.tensor_copy(c_b[:], y_flat[:, 0:896]).then_inc(sm("cast"), 1)
            dve.wait_ge(sm("cast"), 1)
            for i in range(B):
                dve.wait_ge(sm(f"x_in{i}"), 16)
                for u in range(TB):
                    dve_stats(dve, 0, TB * i + u)
            dve_proj(dve, "a")
            dve_attn(dve, "a")
            dve_out(dve, "a")
            dve_ffn(dve, "f")
            dve_proj(dve, "b")
            dve_attn(dve, "b")
            dve_out(dve, "b")
            dve_ffn(dve, "h")

        def pe_transpose_tile(pe, s, t, u):
            dst = t_ps if u % 2 == 0 else o_ps
            pe.wait_ge(sm(s + "_xn"), t + 1)
            for c in range(CE):
                last = pe.transpose(dst[:, c * P:(c + 1) * P], xn[:, u % 2, c * P:(c + 1) * P], ident_f)
            return last

        def pe_proj_tile(pe, s, t, u, ahead):
            if ahead:
                pe_transpose_tile(pe, s, t + 1, u + 1).then_inc(sm(s + "_xt"), 1)
            pe.wait_ge(sm(s + "_xnT"), t + 1)
            pe.wait_ge(sm(s + "_ps_free"), t + 1)
            nqk = 384 if s == "a" else 512
            for c in range(CE):
                mm = pe.matmul(st_ps[:, u % 2, 0:nqk], xnT[:, c, u * P:(u + 1) * P], wqkv[:, c, 0:nqk],
                               start=c == 0, stop=c == CE - 1)
            mm.then_inc(sm(s + "_qkv"), 1)
            if s == "b":
                for c in range(CE):
                    mm = pe.matmul(st_ps[:, u % 2, 512:768], xnT[:, c, u * P:(u + 1) * P], wqkv[:, c, 512:768],
                                   start=c == 0, stop=c == CE - 1)
                mm.then_inc(sm(s + "_qkv"), 1)

        def pe_proj(pe, s):
            pe.sem_inc(sm(s + "_ps_free"), 2)
            pe_transpose_tile(pe, s, 0, 0).then_inc(sm(s + "_xt"), 1)
            with pe.Fori(0, B - 1) as b:
                for u in range(TB):
                    pe_proj_tile(pe, s, TB * b + u, u, True)
            for u in range(TB):
                pe_proj_tile(pe, s, TB * (B - 1) + u, u, u < TB - 1)

        def q_of(g, h, a, b_):
            r = 64 * (h % 2)
            return qT[r:r + W, 2 * g + h // 2, a:b_]

        def k_of(s, g, h, a, b_):
            r = 64 * (h % 2)
            return kT[r:r + W, (2 * g + h // 2) if s == "b" else g, a:b_]

        def pe_unit(pe, s, n, g, u):
            buf = (5 * g + u) % 2
            pe.wait_ge(sm(s + "_exp_done"), 5 * n + u + 1)
            for bank in range(2):
                ps = st_ps[:, buf, 512 * bank:512 * bank + 512]
                if u < 2:
                    h = 2 * u + bank
                    pe.matmul(ps, k_of(s, g, h, 0, P), q_of(g, h, 0, T), start=True, stop=False,
                              skip_group_check=True)
                    mm = pe.matmul(ps[:, 0:P], ident_b, mask_t[:, 0:P], start=False, stop=True, skip_group_check=True)
                elif u < 4:
                    h = 2 * (u - 2) + bank
                    pe.matmul(ps[:, 0:P], k_of(s, g, h, 3 * P, 4 * P), q_of(g, h, 3 * P, T), start=True, stop=False,
                              skip_group_check=True)
                    pe.matmul(ps[:, P:T], k_of(s, g, h, P, 2 * P), q_of(g, h, P, T), start=False, stop=False,
                              skip_group_check=True)
                    mm = pe.matmul(ps[:, 0:2 * P], ident_b, mask_t, start=False, stop=True, skip_group_check=True)
                else:
                    for j in range(2):
                        h = 2 * j + bank
                        pe.matmul(ps[:, 256 * j:256 * j + 256], k_of(s, g, h, 2 * P, 3 * P), q_of(g, h, 2 * P, T),
                                  start=j == 0, stop=False, skip_group_check=True)
                    mm = pe.matmul(ps.rearrange("p (j c) -> p j c", j=2)[:, :, 0:P], ident_b,
                                   mask_t.rearrange("p (j c) -> p j c", j=2), start=False, stop=True,
                                   skip_group_check=True)
            mm.then_inc(sm(s + "_st_done"), 1)

        def pe_scores(pe, s, n, g, k):
            ps = s_ps[:, k % 2, :]
            if k == 0:
                pe.wait_ge(sm(s + "_q_evac"), n + 1)
                pe.wait_ge(sm(s + "_k_evac"), n + 1)
            pe.wait_ge(sm(s + "_max_done"), 10 * n + k + 1)
            if k < 4:
                pe.matmul(ps, q_of(g, k, 3 * P, T), k_of(s, g, k, 0, T), start=True, stop=False, skip_group_check=True)
                mm = pe.matmul(ps[:, 3 * P:T], ident_b, mask_s[:, 0:P], start=False, stop=True, skip_group_check=True)
            elif k < 8:
                h = k - 4
                pe.matmul(ps[:, 0:3 * P], q_of(g, h, 2 * P, 3 * P), k_of(s, g, h, 0, 3 * P), start=True, stop=False,
                          skip_group_check=True)
                pe.matmul(ps[:, 3 * P:T], q_of(g, h, 0, P), k_of(s, g, h, 0, P), start=False, stop=False,
                          skip_group_check=True)
                mm = pe.matmul(ps[:, 2 * P:T], ident_b, mask_s, start=False, stop=True, skip_group_check=True)
            else:
                for j in range(2):
                    h = 2 * j + k - 8
                    pe.matmul(ps[:, 256 * j:256 * j + 256], q_of(g, h, P, 2 * P), k_of(s, g, h, 0, 2 * P),
                              start=j == 0, stop=False, skip_group_check=True)
                mm = pe.matmul(ps.rearrange("p (j c) -> p j c", j=2)[:, :, P:2 * P], ident_b,
                               mask_s.rearrange("p (j c) -> p j c", j=2), start=False, stop=True,
                               skip_group_check=True)
            mm.then_inc(sm(s + "_s_done"), 1)

        def pe_tr_q(pe, s, t, g):
            pe.wait_ge(sm(s + "_split_done"), 2 * t + 1)
            for pr in range(PR):
                for i in range(TB):
                    src = stq[:, g % 2, i * HG + 2 * pr:i * HG + 2 * pr + 2, :].rearrange("p h w -> p (h w)")
                    mm = pe.transpose(t_bf[:, pr * T + i * P:pr * T + (i + 1) * P], src, ident_b)
            mm.then_inc(sm(s + "_tr_done"), 1)

        def pe_tr_k(pe, s, t, g):
            pe.wait_ge(sm(s + "_split_done"), 2 * t + 2)
            pe.wait_ge(sm(s + "_q_evac"), t + 1)
            for pr in range(PR if s == "b" else 1):
                for i in range(TB):
                    src = stk[:, g % 2, i * HG + 2 * pr:i * HG + 2 * pr + 2, :].rearrange("p h w -> p (h w)")
                    mm = pe.transpose(t_bf[:, pr * T + i * P:pr * T + (i + 1) * P], src, ident_b)
            mm.then_inc(sm(s + "_tr_done"), 1)

        def pe_m_tr(pe, s, hp):
            hold(pe, s + "_m_split", hp + 1)
            for i in range(TB):
                mm = pe.transpose(t_bf[0:48, i * P:(i + 1) * P], ms[:, i].rearrange("p c h -> p (c h)"), ident_b)
            mm.then_inc(sm(s + "_m_tr"), 1)

        def pe_pv(pe, s, n, g, u, j, last=False):
            vw = 9 if s == "a" else 17
            for h in range(HG):
                v = v_b[:, g, j, 0:9] if s == "a" else v_b[:, g, j, 17 * (h // 2):17 * (h // 2) + 17]
                if j == 0:
                    r, a, c = 5 * g + h // 2, 512 * (h % 2), 512
                elif j == 1:
                    r, a, c = 5 * g + 2 + h // 2, 512 * (h % 2) + P, 384
                elif j == 3:
                    r, a, c = 5 * g + 2 + h // 2, 512 * (h % 2), P
                else:
                    r, a, c = 5 * g + 4, 512 * (h % 2) + 256 * (h // 2), 256
                mm = pe.matmul(o_ps[32 * h:32 * h + vw, T - c:T], v, p_ring[:, r % RING, a:a + c], start=j == 0,
                               stop=last, tile_position=(0, 32 * h), skip_group_check=True)
            return mm

        def pe_slot(pe, s, n, g, b, with_s, with_t):
            sn, sg = n + 7, (g - 1) % G

            def scores(*ks):
                if with_s:
                    for k in ks:
                        pe_scores(pe, s, sn, sg, k)

            if g % 4 == 0:
                pe.wait_ge(sm(s + "_m_rows"), M_DMAS * (2 * b + 1 + g // 4))
            pe_unit(pe, s, n, g, 0)
            pe_unit(pe, s, n, g, 1)
            pe.wait_ge(sm(s + "_norm_done"), n + 1)
            m_now = g == 1 or (g == 5 and with_t)
            if m_now:
                pe_m_tr(pe, s, 2 * b + (1 if g == 1 else 2))
            scores(0, 1)
            pe_unit(pe, s, n, g, 2)
            scores(2, 3)
            pe.wait_ge(sm(s + "_v_done"), n + 1)
            pe.wait_ge(sm(s + "_exp_done"), 5 * n + 4)
            pe_pv(pe, s, n, g, 0, 0).then_inc(sm(s + "_p_free"), 2)
            pe_unit(pe, s, n, g, 3)
            scores(4, 5)
            pe_unit(pe, s, n, g, 4)
            if m_now:
                pe.wait_ge(sm(s + "_m_evac"), 2 * b + (2 if g == 1 else 3))
            if with_t:
                pe_tr_q(pe, s, n + 8, g)
            scores(6)
            pe.wait_ge(sm(s + "_exp_done"), 5 * n + 6)
            pe_pv(pe, s, n, g, 2, 1)
            pe_pv(pe, s, n, g, 2, 3).then_inc(sm(s + "_p_free"), 2)
            if with_t:
                pe_tr_k(pe, s, n + 8, g)
            scores(7, 8)
            pe.wait_ge(sm(s + "_exp_done"), 5 * n + 7)
            pe_pv(pe, s, n, g, 4, 2, last=True).then_inc(sm(s + "_p_free"), 1)
            scores(9)
            if with_t:
                pe.wait_ge(sm(s + "_k_evac"), n + 9)
            pe.wait_ge(sm(s + "_ot_evac"), n + 1)
            for i in range(TB):
                mm = pe.transpose(t_ps[:, i * P:(i + 1) * P], oT_sb[:, i * P:(i + 1) * P], ident_f)
            mm.then_inc(sm(s + "_otr_done"), 1)

        def pe_attn(pe, s):
            pe.sem_inc(sm(s + "_p_free"), RING)
            pe.wait_ge(sm(s + "_o_init"), 1)
            if s == "a":
                pe.wait_ge(sm("cast"), 1)
            pe_tr_q(pe, s, 0, 0)
            pe_tr_k(pe, s, 0, 0)
            for g in range(G - 1):
                pe.wait_ge(sm(s + "_k_evac"), g + 1)
                if g == 4:
                    pe_m_tr(pe, s, 0)
                for k in range(SBANKS):
                    pe_scores(pe, s, g, g, k)
                if g == 4:
                    pe.wait_ge(sm(s + "_m_evac"), 1)
                pe_tr_q(pe, s, g + 1, g + 1)
                pe_tr_k(pe, s, g + 1, g + 1)
            pe.wait_ge(sm(s + "_k_evac"), G)
            with pe.Fori(0, B - 1) as b:
                for g in range(G):
                    pe_slot(pe, s, 8 * b + g, g, b, True, True)
            for g in range(G):
                pe_slot(pe, s, 8 * (B - 1) + g, g, B - 1, g == 0, False)

        def pe_out(pe, s):
            pe.wait_ge(sm(s + "_norm_done"), 1 + B * G)
            for t in range(NT + 1):
                if t < NT:
                    if s == "b":
                        pe.wait_ge(sm("b_y"), t + 1)
                    if t >= 2:
                        pe.wait_ge(sm(s + "_yT"), t - 1)
                    for c in range(CE):
                        mm = pe.transpose((t_ps if t % 2 == 0 else o_ps)[:, c * P:(c + 1) * P],
                                          y_sb[:, t, c * P:(c + 1) * P], ident_f)
                    mm.then_inc(sm(s + "_yt"), 1)
                if t >= 1:
                    n = t - 1
                    pe.wait_ge(sm(s + "_yT"), n + 1)
                    if n >= 4:
                        pe.wait_ge(sm(s + "_out_x"), n - 3)
                    for c in range(CE):
                        mm = pe.matmul(out_ps(n), xnT[:, c, n % 4 * P:n % 4 * P + P], wo[:, c, :], start=c == 0,
                                       stop=c == CE - 1)
                    mm.then_inc(sm(s + "_po"), 1)

        def pe_ffn(pe, f):
            pe.sem_inc(sm(f + "_sil_free"), 2)
            pe.sem_inc(sm(f + "_hw_used"), 2)
            pe.wait_ge(sm("g_w"), 16)

            def logits(t):
                pe.wait_ge(sm("e_xnT"), t + 1 + past(f, NT))
                for c in range(CE):
                    mm = pe.matmul(logits_ps(t // TH)[:, t % TH * NE:t % TH * NE + NE], xnT_all[:, c, t * P:(t + 1) * P], wg[:, c, :],
                                   start=c == 0, stop=c == CE - 1)
                if t % TH == TH - 1:
                    mm.then_inc(sm("e_lg"), 1)

            for t in range(NT):
                dst = t_ps if t % 2 == 0 else o_ps
                pe.wait_ge(sm("e_xn"), t + 1 + past(f, NT))
                if t >= 2:
                    pe.wait_ge(sm("e_xnT"), t - 1 + past(f, NT))
                for c in range(CE):
                    mm = pe.transpose(dst[:, c * P:(c + 1) * P], y_sb[:, t, c * P:(c + 1) * P], ident_f)
                mm.then_inc(sm("e_xt"), 1)
                if t >= 1:
                    logits(t - 1)
            logits(NT - 1)
            pe.wait_ge(sm(f + "_w"), 4 * 16)

            def counts(hf):
                pe.wait_ge(sm("e_taken"), hf + 1 + past(f, 2))
                a = taken[:].rearrange("p t e -> p (t e)")
                pe.matmul(s_ps[:, 1, 0:P], upper, a, start=True, stop=True, skip_group_check=True)
                pe.matmul(s_ps[:, 1, P:2 * P], ones, a, start=False, stop=True, skip_group_check=True)\
                    .then_inc(sm("e_counts"), 1)

            def shared_in(k):
                b, (r, m) = k // 3, SCH[k % 3]
                pe.wait_ge(sm(f + "_sil_free"), k + 1)
                for a in range(2):
                    for e in range(CE):
                        mm = pe.matmul(st_ps[0:m, k % 2, 512 * a:512 * a + 512], ws13[:, a, e, r:r + m],
                                       xnT_all[:, e, b * T:(b + 1) * T], start=e == 0, stop=e == CE - 1)
                mm.then_inc(sm("e_h"), 1)

            def shared_out(k):
                b, c, m = k // 3, k % 3, SCH[k % 3][1]
                pe.wait_ge(sm(f + "_sil_free"), k + 3)
                if c == 0 and b > 0:
                    pe.wait_ge(sm("e_z_free"), TB * b + past(f, NT))
                for u in range(TB):
                    mm = pe.matmul((t_ps if u < 2 else o_ps)[:, (u % 2) * E:(u % 2) * E + E],
                                   hw[0:m, k % 2, u * P:(u + 1) * P], ws2[0:m, c, :],
                                   start=c == 0 and u % 2 == 0, stop=c == 2, skip_group_check=True)
                mm.then_inc(sm(f + "_hw_used"), 1)

            shared_in(0)
            shared_in(1)
            counts(0)
            for k in range(3 * B):
                if k == 5:
                    counts(1)
                shared_out(k)
                if k + 2 < 3 * B:
                    shared_in(k + 2)

            def turn_in(j, q):
                hold(pe, f"load{q % 4}", 4 * (j - q % 4) + 16 + past(f, 16 * NJ // 4))
                for c in range(CE):
                    mm = pe.transpose((t_ps if q % 2 == 0 else o_ps)[:, c * P:(c + 1) * P],
                                      xg[:, q % 4, c * P:(c + 1) * P], ident_f)
                mm.then_inc(sm("e_x_tr"), 1)

            def expert(j):
                return pe.value_load(tile_e[0:1, ds(j, 1)], min_val=0, max_val=NE - 1)

            def first_layer(j, q, e):
                pe.wait_ge(sm("e_x_ev"), j + 1 + past(f, NJ))
                for c in range(CE):
                    mm = pe.matmul(s_ps[:, q % 2, 0:2 * INTER], xgT[:, q % 2, c, :],
                                   w13[:, c, ds(e, 1), :].rearrange("p a i -> p (a i)"), start=c == 0, stop=c == CE - 1)
                mm.then_inc(sm("e_h1"), 1)

            def turn_inner(j, q):
                pe.wait_ge(sm("e_hs"), j + 1 + past(f, NJ))
                for c in range(2):
                    mm = pe.transpose(st_ps[:, q % 2, c * P:(c + 1) * P], hs[:, q % 2, c * P:(c + 1) * P], ident_f)
                mm.then_inc(sm("e_h_tr"), 1)

            def second_layer(j, q, e):
                pe.wait_ge(sm("e_hT_ev"), j + 1 + past(f, NJ))
                for c in range(2):
                    mm = pe.matmul(st_ps[:, q % 2, 512:512 + E], hsT[:, q % 2, c, :],
                                   w2[:, c, ds(e, 1), :].rearrange("p a d -> p (a d)"), start=c == 0, stop=c == 1)
                mm.then_inc(sm("e_y_mm"), 1)

            pe.wait_ge(sm(f + "_we"), 4 * 16)
            pe.wait_ge(sm("e_hs0"), 1 + past(f, 1))
            turn_in(0, 0)
            turn_in(1, 1)
            first_layer(0, 0, expert(0))
            with pe.Fori(0, NJ // 8 - 1) as i:
                e = [expert(8 * i), expert(8 * i + 1)]
                for q in range(8):
                    j = 8 * i + q
                    turn_in(j + 2, q + 2)
                    turn_inner(j, q)
                    first_layer(j + 1, q + 1, e[q + 1])
                    if q < 7:
                        e.append(expert(j + 2))
                    second_layer(j, q, e[q])
            e = [expert(NJ - 8), expert(NJ - 7)]
            for q in range(8):
                j = NJ - 8 + q
                if q < 6:
                    turn_in(j + 2, q + 2)
                turn_inner(j, q)
                if q < 7:
                    first_layer(j + 1, q + 1, e[q + 1])
                if q < 6:
                    e.append(expert(j + 2))
                second_layer(j, q, e[q])

        @block.tensor
        def _(pe):
            pe.wait_ge(sm("consts"), 16)
            pe.wait_ge(sm("a_w"), 64)
            pe_proj(pe, "a")
            pe_attn(pe, "a")
            pe_out(pe, "a")
            pe_ffn(pe, "f")
            pe.wait_ge(sm("b_w"), 112)
            pe_proj(pe, "b")
            pe_attn(pe, "b")
            pe_out(pe, "b")
            pe_ffn(pe, "h")


def constants():
    pos = np.arange(T, dtype=np.float32) + np.float32(1)
    theta = (10000.0 ** (-2.0 * np.arange(D // 2) / D)).astype(np.float32)
    ang = (pos[:, None] * theta[None, :]).astype(np.float32).reshape(TB, P, D // 2).transpose(1, 0, 2)
    cos, sin = np.cos(ang), np.sin(ang)
    i4, i16 = np.arange(4), np.arange(NE)
    c_f = np.concatenate([
        np.eye(P), np.concatenate([cos, cos], 2).reshape(P, -1), np.concatenate([sin, -sin], 2).reshape(P, -1),
        np.tile((i4[None, :] < i4[:, None]).reshape(1, -1), (P, 1)),
        np.tile((i16[None, :] < i16[:, None]).reshape(1, -1), (P, 1)), 
        np.tile(np.concatenate([np.arange(TH) * P, np.arange(SLOTS), np.arange(TOPK)])[None, :], (P, 1))], 1)\
        .astype(np.float32)
    r = np.arange(P)
    ms = np.where(r[None, :] > r[:, None], MASK, 0.0)
    mt = np.where(r[:, None] > r[None, :], MASK, 0.0)
    c_b = np.concatenate([np.eye(P), ms, ms, mt, mt, r[:, None] < r[None, :], np.ones((P, P))], 1).astype(np.float32)
    return {"c_f": c_f, "c_b": c_b}


def kernel(L0_attn_a_x, L0_attn_a_Wq, L0_attn_a_bq, L0_attn_a_Wk, L0_attn_a_bk, L0_attn_a_Wv, L0_attn_a_bv,
           L0_attn_a_Wo, L0_attn_a_bo, L0_attn_b_Wq, L0_attn_b_Wk, L0_attn_b_Wv, L0_attn_b_Wo, L0_attn_b_lambda_q1,
           L0_attn_b_lambda_k1, L0_attn_b_lambda_q2, L0_attn_b_lambda_k2, L0_attn_b_subln_weight, L0_ffn_Wg,
           L0_ffn_W1, L0_ffn_W3, L0_ffn_W2, L0_ffn_Ws1, L0_ffn_Ws3, L0_ffn_Ws2):
    import concourse.bacc as bacc
    from concourse.bass_utils import run_bass_kernel_spmd as run

    n = np.asarray
    arrays = {
        "x": n(L0_attn_a_x),
        "a_wqkv": np.concatenate([n(L0_attn_a_Wq).T, n(L0_attn_a_Wk).T, n(L0_attn_a_Wv).T], 1),
        "a_bqkv": np.concatenate([n(L0_attn_a_bq), n(L0_attn_a_bk), n(L0_attn_a_bv)]),
        "a_wo": n(L0_attn_a_Wo).T, "a_bo": n(L0_attn_a_bo),
        "b_wqkv": np.concatenate([n(L0_attn_b_Wq).T, n(L0_attn_b_Wk).T, n(L0_attn_b_Wv).T], 1),
        "b_wo": n(L0_attn_b_Wo).T, "b_g": n(L0_attn_b_subln_weight),
        "b_lq1": n(L0_attn_b_lambda_q1), "b_lk1": n(L0_attn_b_lambda_k1),
        "b_lq2": n(L0_attn_b_lambda_q2), "b_lk2": n(L0_attn_b_lambda_k2),
        "wg": n(L0_ffn_Wg).T,
        "w13": np.concatenate([n(L0_ffn_W1).transpose(2, 0, 1), n(L0_ffn_W3).transpose(2, 0, 1)], 2),
        "w2": np.concatenate([n(L0_ffn_W2).transpose(0, 2, 1), np.zeros((NE, 2 * P - INTER, E), np.float32)], 1),
        "ws1": n(L0_ffn_Ws1).T, "ws3": n(L0_ffn_Ws3).T, "ws2": n(L0_ffn_Ws2).T,
    }
    arrays |= constants()
    arrays = {k: np.ascontiguousarray(v) for k, v in arrays.items()}
    nc = bacc.Bacc("TRN2", target_bir_lowering=False, num_devices=1)
    ins = {k: nc.dram_tensor("in_" + k, v.shape, mybir.dt.from_np(v.dtype), kind="ExternalInput").ap()
           for k, v in arrays.items()}
    out = nc.dram_tensor("out_0", (B, T, E), F32, kind="ExternalOutput").ap()
    build(nc, ins, out)
    r = run(nc, [{"in_" + k: v for k, v in arrays.items()}], core_ids=[0])
    return r.results[0]["out_0"]
```
